# Optimizing a Trainium2 kernel written in Bass

```python
import numpy as np
import jax
import jax.numpy as jnp

def _softmax(x, axis=-1):
    return jax.nn.softmax(x, axis=axis)

def _gelu(x):
    return jax.nn.gelu(x, approximate=True)

def _silu(x):
    return jax.nn.silu(x)

def _sigmoid(x):
    return jax.nn.sigmoid(x)

def _layernorm(x, axis=-1, eps=1e-05):
    m = jnp.mean(x, axis=axis, keepdims=True)
    v = jnp.var(x, axis=axis, keepdims=True)
    return (x - m) / jnp.sqrt(v + eps)

def _scatter_add(tgt, idx, src, axis=0):
    return tgt.at[idx].add(src)

def _segment_sum(src, seg, n):
    return jax.ops.segment_sum(src, seg, n)
kernel_name = 'mk_adj_preln_d2_adj_r2_103d2d'

def setup_inputs(seed: int=0):
    np.random.seed(seed)
    _w = jnp.asarray

    def _rec_inputs():
        import jax
        import jax.numpy as jnp
        _gk = jax.random.key(seed)
        x = -0.000929 + 1 * jax.random.normal(jax.random.fold_in(_gk, 1), (4096, 128), jnp.float32)
        _w = (1.0 + jnp.arange(4096, dtype=jnp.float32)) ** (-0.5)
        _w = _w / _w.mean()
        _pij = jnp.clip(0.000976562 * _w[:, None] * _w[None, :], 0.0, 1.0)
        _a = jax.random.uniform(jax.random.fold_in(_gk, 2), (4096, 4096)) < _pij
        _a = jnp.logical_or(_a, jnp.eye(4096, dtype=bool))
        _af = _a.astype(jnp.float32)
        adj = _af
        return (x, adj)
    x, adj = _rec_inputs()

    def _L0_gnn_setup():
        import jax, jax.numpy as jnp
        import numpy as np
        N = 4096
        D = 128
        EDGE_P = 0.005
        key = jax.random.key(seed)
        kx, ka, kb = jax.random.split(key, 3)
        x = jax.random.normal(kx, (N, D), dtype=jnp.float32)
        adj = (jax.random.uniform(ka, (N, N)) < EDGE_P).astype(jnp.float32)
        adj = jnp.maximum(adj, jnp.eye(N, dtype=jnp.float32))
        beta = jax.random.uniform(kb, (1,), dtype=jnp.float32)
        return {'x': x, 'adj': adj, 'beta': beta}
    _L0_gnn_all = _L0_gnn_setup()
    _L0_gnn_in = {k: v for k, v in _L0_gnn_all.items() if k in ('beta',)}
    del _L0_gnn_all

    def _L1_gnn_setup():
        import jax, jax.numpy as jnp
        import numpy as np
        key = jax.random.key(seed)
        k1, k2, k3, k4 = jax.random.split(key, 4)
        n, in_dim, out_dim = (8192, 128, 128)
        h = jax.random.normal(k1, (n, in_dim), dtype=jnp.float32)
        adj = jax.random.uniform(k2, (n, n), dtype=jnp.float32)
        W_self = jax.random.normal(k3, (in_dim, out_dim), dtype=jnp.float32) * (1.0 / np.sqrt(in_dim))
        W_neigh = jax.random.normal(k4, (in_dim, out_dim), dtype=jnp.float32) * (1.0 / np.sqrt(in_dim))
        return {'h': h, 'adj': adj, 'W_self': W_self, 'W_neigh': W_neigh}
    _L1_gnn_all = _L1_gnn_setup()
    _L1_gnn_in = {k: v for k, v in _L1_gnn_all.items() if k in ('W_self', 'W_neigh')}
    del _L1_gnn_all
    return {'x': x, 'adj': adj, 'L0_gnn_beta': _L0_gnn_in['beta'], 'L1_gnn_W_self': _L1_gnn_in['W_self'], 'L1_gnn_W_neigh': _L1_gnn_in['W_neigh']}

def reference(x, adj, L0_gnn_beta, L1_gnn_W_self, L1_gnn_W_neigh):
    import jax
    import jax.numpy as jnp

    def _L0_gnn_ref(x, adj, beta):
        import jax, jax.numpy as jnp
        import numpy as np
        N = 4096
        D = 128
        EDGE_P = 0.005
        norm2 = jnp.linalg.norm(x, axis=1, keepdims=True)
        cos = beta[0] * (x @ x.T) / (norm2 @ norm2.T + 1e-07)
        masked = cos + (1.0 - adj) * -1000000000.0
        P = jax.nn.softmax(masked, axis=1)
        return P @ x

    def _L1_gnn_ref(h, adj, W_self, W_neigh):
        import jax, jax.numpy as jnp
        import numpy as np
        deg = jnp.clip(jnp.sum(adj, axis=1, keepdims=True), 1.0)
        h_neigh = adj @ h / deg
        return h @ W_self + h_neigh @ W_neigh
    h = jnp.maximum(_layernorm(x, axis=-1), 0.0)
    x = x + _L0_gnn_ref(h, adj, L0_gnn_beta)
    h = jnp.maximum(_layernorm(x, axis=-1), 0.0)
    x = x + _L1_gnn_ref(h, adj, L1_gnn_W_self, L1_gnn_W_neigh)
    return x

_drawn_inputs = setup_inputs


def setup_inputs(seed=0):
    import zlib

    import numpy as np

    out = dict(_drawn_inputs(seed))
    spreads = {}
    factors = {}
    for name, (base, spread) in spreads.items():
        noise = np.random.default_rng([zlib.crc32(name.encode()), seed]).standard_normal(out[name].shape)
        drawn = base * np.exp(spread * noise) if base else spread * noise
        out[name] = jnp.asarray(drawn.astype(out[name].dtype))
    for name, factor in factors.items():
        out[name] = (out[name] * factor).astype(out[name].dtype)
    return out
```

```python
import concourse.bass as bass
from concourse import mybir
from contextlib import ExitStack


def gnn_program(nc, x_in, adj_in, beta_in, w_self_in, w_neigh_in, out):
    fp32, fp16, bf16, fp8 = mybir.dt.float32, mybir.dt.float16, mybir.dt.bfloat16, mybir.dt.float8e4
    u8 = mybir.dt.uint8
    ALU, ACT = mybir.AluOpType, mybir.ActivationFunctionType

    N, D = x_in.shape
    P = 128
    T = N // P
    ROWS = 512
    TPS = ROWS // P
    NS = N // ROWS
    PAIRS = T // 2
    PIECES = PAIRS // 2
    PW = 4 * P
    UNROLL = 4
    HS = 256.0
    GS = 16.0
    E_BITS = 14
    LN2 = 0.6931471805599453
    MASK = 2.0 ** 30
    EPS = 1e-5
    FP8_ONE, FP8_MINUS_ONE = 0x38, 0xB8
    TW = 2 * D + 1

    x_v = x_in.rearrange("(t p) d -> p t d", p=P)
    out_v = out.rearrange("(t p) d -> p t d", p=P)
    adj_v = adj_in.rearrange("(t p) j -> p t j", p=P)

    ctx = ExitStack()
    with ctx:
        def sb(name, shape, dt):
            return ctx.enter_context(nc.sbuf_tensor(name, shape, dt))

        def sem(name):
            return ctx.enter_context(nc.semaphore(name))

        adj_tb = sb("adj_t", [P, NS * T * ROWS], u8)
        x_sb = sb("x_sb", [P, T * D], fp32)
        table = sb("table", [P, T * TW], fp16)
        unit_t = sb("unit_t", [P, 2 * N], fp16)
        stage = sb("stage", [P, 2 * TPS * PW], fp32)
        adjm1b = sb("adjm1", [P, 2 * TPS * PW], u8)
        e_hi = sb("e_hi", [P, 2 * 2 * ROWS], fp16)
        e_lo = sb("e_lo", [P, 2 * 2 * ROWS], fp16)
        small = sb("small", [P, 96], fp32)
        mask_id = sb("mask_id", [P, P], bf16)
        mean_h = sb("mean_h", [P, D], fp32)
        zeros_w = sb("zeros_w", [P, P], fp16)
        ps = ctx.enter_context(nc.psum_tensor("ps", [P, 8, 512], fp32))

        adj_t = adj_tb[:, :].bitcast(fp8)
        adjm1 = adjm1b[:, :].bitcast(fp8)

        h_f = adj_t[:, 0:T * D * 4].bitcast(fp32)
        u_f = adj_t[:, T * D * 4:2 * T * D * 4].bitcast(fp32)
        o0 = 2 * T * D * 4
        stats = adj_t[:, o0:o0 + T * 6 * 4].bitcast(fp32)
        o1 = o0 + T * 6 * 4
        ident = adj_t[:, o1:o1 + P * 4].bitcast(fp32)
        o2 = o1 + P * 4
        ones_w = adj_t[:, o2:o2 + P * 2].bitcast(fp16)
        o3 = o2 + P * 2
        mv = adj_t[:, o3:o3 + T * 2 * 4].bitcast(fp32)
        o4 = o3 + T * 2 * 4
        vec = [adj_t[:, o4 + i * T * 4:o4 + (i + 1) * T * 4].bitcast(fp32) for i in range(6)]
        o5 = o4 + 6 * T * 4

        h2_f = unit_t[:, :].bitcast(fp32)
        w_cat = stage[:, 0:2 * D]
        ident2 = stage[:, 256:384]
        h2_t = [stage[:, 512 + 512 * i:1024 + 512 * i] for i in range(2)]
        stats2 = stage[:, 1536:1536 + T * 6]
        mv2 = stage[:, 1792:1792 + 2 * T]
        vec2 = [stage[:, 1920 + T * i:1920 + T * (i + 1)] for i in range(6)]

        beta = small[:, 0:1]
        beta_s = small[:, 1:2]
        exp_scale = small[:, 2:3]
        exp_bias = small[:, 3:4]
        b_sq = small[:, 4:5]
        b_zero = small[:, 5:6]
        b_inv = small[:, 6:7]
        b_keep = small[:, 7:8]
        b_pos = small[:, 8:9]
        no_edge = small[:, 16:20]
        den_s = small[:, 20:24]
        rden = small[:, 24:28]

        def tab(t, lo=0, hi=TW):
            return table[:, t * TW + lo:t * TW + hi]

        s_x = [sem(f"x_loaded{i}") for i in range(4)]
        s_beta = sem("beta_loaded")
        s_w = sem("weights_loaded")
        s_stage = [sem(f"stage_loaded{i}") for i in range(2)]
        s_out = sem("out_stored")
        s_ident = sem("ident_ready")
        s_step = sem("dve_step")
        s_maskid = sem("mask_identity_ready")
        s_rvar = sem("rvar_ready")
        s_sqrt = sem("sqrt_ready")
        s_rstd = sem("rstd_ready")
        s_h = sem("h_ready")
        s_unit = sem("unit_ready")
        s_tp = sem("transposed")
        s_uhi = sem("unit_hi_ready")
        s_ulo = sem("unit_lo_ready")
        s_hh = sem("table_high_ready")
        s_tab = sem("table_ready")
        s_cs = sem("colsum_ready")
        s_first = sem("constants_ready")
        s_adjm1 = sem("adjm1_ready")
        s_scores = sem("scores_ready")
        s_ehi = sem("exp_hi_ready")
        s_exp = sem("exp_ready")
        s_elo = sem("exp_lo_ready")
        s_adjt = sem("adj_t_ready")
        s_pv = sem("pv_done")
        s_evac = sem("acc_evacuated")
        s_evs = sem("evacuation_step")
        s_h2 = sem("h2_ready")
        s_h2p = sem("h2_transposed")
        s_h2t = sem("h2_t_ready")
        s_g = sem("g_ready")
        s_ghi = sem("g_hi_ready")
        s_gtab = sem("g_table_ready")
        s_step2 = sem("dve_step2")
        s_rvar2 = sem("rvar2_ready")
        s_sqrt2 = sem("sqrt2_ready")
        s_rstd2 = sem("rstd2_ready")
        s_agg = sem("agg_ready")
        s_aggfree = sem("agg_bank_free")
        s_res = sem("result_ready")
        s_ident2 = sem("ident2_ready")
        CREDIT = 2

        block = ctx.enter_context(nc.Block())

        @block.sync
        def _(sp):
            sp.dma_start(beta, beta_in.partition_broadcast(P)).then_inc(s_beta, 16)
            for i in range(4):
                sp.dma_start(x_sb[:, i * 8 * D:(i + 1) * 8 * D].rearrange("p (t d) -> p t d", d=D),
                             x_v[:, 8 * i:8 * i + 8, :]).then_inc(s_x[i], 16)
            with sp.Fori(0, NS) as s:
                with sp.Fori(0, PIECES // 2) as q:
                    for i in range(2):
                        sp.wait_ge(s_adjm1, s * PIECES + q * 2 + (i + 1))
                        sp.dma_start(stage[:, i * TPS * PW:(i + 1) * TPS * PW].rearrange("p (t c) -> p t c", c=PW),
                                     adj_v[:, bass.ds(s * TPS, TPS), bass.ds(q * 2 * PW + i * PW, PW)]
                                     ).then_inc(s_stage[i], 16)
            sp.wait_ge(s_adjm1, NS * PIECES + CREDIT)
            sp.dma_start(w_cat[:, 0:D], w_neigh_in).then_inc(s_w, 16)
            sp.dma_start(w_cat[:, D:2 * D], w_self_in).then_inc(s_w, 16)
            for g in range(NS):
                sp.wait_ge(s_res, g + 1)
                sp.dma_start(out_v[:, g * TPS:(g + 1) * TPS, :],
                             x_sb[:, g * ROWS:(g + 1) * ROWS].rearrange("p (t d) -> p t d", d=D)).then_inc(s_out, 16)
            sp.wait_ge(s_out, 16 * NS)

        @block.gpsimd
        def _(pool):
            pool.memset(ident, 0.0).then_inc(s_ident, 1)
            pool.memset(ones_w, 1.0).then_inc(s_first, 1)
            pool.memset(zeros_w[:, :], 0.0).then_inc(s_first, 1)
            pool.memset(table[:, :].rearrange("p (t w) -> p t w", w=TW)[:, :, 2 * D:TW], 1.0).then_inc(s_first, 1)
            pool.wait_ge(s_ident, 1)
            pool.affine_select(out=ident, in_=ident, compare_op=ALU.not_equal, fill=1.0, base=0,
                               pattern=[[-1, P]], channel_multiplier=1).then_inc(s_ident, 1)
            tv = table[:, :].rearrange("p (t w) -> p t w", w=TW)
            hv = h_f.rearrange("p (t d) -> p t d", d=D)
            for g in range(NS):
                pool.wait_ge(s_h, (g + 1) * TPS)
                a, b = g * TPS, (g + 1) * TPS
                pool.tensor_copy(tv[:, a:b, D:2 * D], hv[:, a:b, :]).then_inc(s_hh, 1)
                pool.wait_ge(s_hh, g + 1)
                pool.tensor_tensor(tv[:, a:b, 0:D], hv[:, a:b, :], tv[:, a:b, D:2 * D], ALU.subtract
                                   ).then_inc(s_tab, 1)
            pool.wait_ge(s_adjm1, NS * PIECES + CREDIT)
            pool.memset(ident2, 0.0).then_inc(s_ident2, 1)
            pool.wait_ge(s_ident2, 1)
            pool.affine_select(out=ident2, in_=ident2, compare_op=ALU.not_equal, fill=1.0, base=0,
                               pattern=[[-1, P]], channel_multiplier=1).then_inc(s_ident2, 1)

        @block.scalar
        def _(act):
            act.wait_ge(s_rvar, 1)
            act.activation(vec[1], vec[0], ACT.Sqrt).then_inc(s_sqrt, 1)
            act.wait_ge(s_rstd, 1)
            for t in range(T):
                act.activation(h_f[:, t * D:(t + 1) * D], x_sb[:, t * D:(t + 1) * D], ACT.Relu,
                               bias=vec[3][:, t:t + 1], scale=vec[2][:, t:t + 1]).then_inc(s_h, 1)
            act.wait_ge(s_rvar, 2)
            act.activation(vec[1], vec[0], ACT.Sqrt).then_inc(s_sqrt, 1)
            for g in range(NS):
                act.wait_ge(s_tp, g + 1)
                act.activation(unit_t[:, g * ROWS:(g + 1) * ROWS], ps[:, 4 + g % 4, :], ACT.Copy).then_inc(s_uhi, 1)

            with act.Fori(0, NS) as s:
                with act.Fori(0, PAIRS // UNROLL) as k:
                    for u in range(UNROLL):
                        n = s * PAIRS + k * UNROLL + u
                        bank = 4 + 2 * (u % 2)
                        hi = e_hi[:, (u % 2) * 2 * ROWS:(u % 2 + 1) * 2 * ROWS]
                        sc = ps[:, bank:bank + 2, :].rearrange("p a b -> p (a b)")
                        act.wait_ge(s_scores, n + 2)
                        act.wait_ge(s_pv, n + 1)
                        act.wait_ge(s_adjt, n + 1)
                        act.activation(hi, sc, ACT.Exp, bias=exp_bias, scale=exp_scale).then_inc(s_ehi, 1)
                        act.activation(sc, sc, ACT.Exp, bias=exp_bias, scale=exp_scale).then_inc(s_exp, 1)

            act.wait_ge(s_rvar2, 1)
            act.activation(vec2[1], vec2[0], ACT.Sqrt).then_inc(s_sqrt2, 1)
            act.wait_ge(s_rstd2, 1)
            for t in range(T):
                act.activation(h2_f[:, t * D:(t + 1) * D], x_sb[:, t * D:(t + 1) * D], ACT.Relu,
                               bias=vec2[3][:, t:t + 1], scale=vec2[2][:, t:t + 1]).then_inc(s_h2, 1)
            for g in range(NS):
                act.wait_ge(s_h2p, g + 1)
                if g >= 2:
                    act.wait_ge(s_g, g - 1)
                act.activation(h2_t[g % 2], ps[:, 6 + g % 2, :], ACT.Copy).then_inc(s_h2t, 1)
                act.wait_ge(s_g, g + 1)
                gp = ps[:, 2 * (g % 2):2 * (g % 2) + 2, :].rearrange("p a (b c) -> p (a b) c", b=2)
                tv = table[:, :].rearrange("p (t w) -> p t w", w=TW)
                act.activation(tv[:, g * TPS:(g + 1) * TPS, D:2 * D], gp[:, :, 0:D], ACT.Copy).then_inc(s_ghi, 1)

        @block.vector
        def _(dve):
            steps = [0]

            def then(ins, counter=s_step):
                steps[0] += 1
                ins.then_inc(counter, 1)
                dve.wait_ge(counter, steps[0])

            dve.wait_ge(s_beta, 16)
            then(dve.tensor_tensor(b_sq, beta, beta, ALU.mult))
            then(dve.tensor_scalar(b_zero, b_sq, 1e-36, 1e-18, ALU.is_le, ALU.mult))
            then(dve.tensor_scalar(b_keep, b_sq, 1e-36, None, ALU.is_gt))
            then(dve.scalar_tensor_tensor(beta_s, beta, b_keep, b_zero, ALU.mult, ALU.add))
            then(dve.reciprocal(b_inv, beta_s))
            then(dve.tensor_scalar(exp_scale, beta_s, 1.0 / (HS * HS), None, ALU.mult))
            then(dve.tensor_scalar(b_pos, beta, 0.0, None, ALU.max))
            then(dve.tensor_scalar(exp_bias, b_pos, -1.0, E_BITS * LN2, ALU.mult, ALU.add))
            dve.wait_ge(s_ident, 2)
            dve.tensor_scalar(mask_id[:, :], ident, b_inv, MASK * HS * HS, ALU.mult, ALU.mult).then_inc(s_maskid, 1)

            def row_scales(x_part, st, m, v, scale, counter, rvar, sq, sq_at, rstd):
                for t in range(T):
                    if x_part is not None and t % 8 == 0:
                        dve.wait_ge(x_part[t // 8], 16)
                    last = dve.bn_stats(st[:, t * 6:(t + 1) * 6], x_sb[:, t * D:(t + 1) * D])
                then(last, counter)
                for t in range(T):
                    last = dve.bn_aggr(m[:, t * 2:(t + 1) * 2], st[:, t * 6:(t + 1) * 6])
                then(last, counter)
                mm = m.rearrange("p (t c) -> p t c", c=2)
                then(dve.tensor_scalar(v[4], mm[:, :, 1], EPS, None, ALU.add), counter)
                dve.reciprocal(v[0], v[4]).then_inc(rvar, 1)
                dve.wait_ge(sq, sq_at)
                newton(v, scale, counter)
                dve.scalar_tensor_tensor(v[3], mm[:, :, 0], -1.0, v[2], ALU.mult, ALU.mult).then_inc(rstd, 1)

            def newton(v, scale, counter):
                then(dve.tensor_tensor(v[5], v[1], v[1], ALU.mult), counter)
                then(dve.tensor_tensor(v[0], v[5], v[4], ALU.mult), counter)
                then(dve.tensor_scalar(v[5], v[0], -0.5 * scale, 1.5 * scale, ALU.mult, ALU.add), counter)
                then(dve.tensor_tensor(v[2], v[5], v[1], ALU.mult), counter)

            row_scales(s_x, stats, mv, vec, HS, s_step, s_rvar, s_sqrt, 1, s_rstd)
            for t in range(T):
                dve.wait_ge(s_h, t + 1)
                last = dve.tensor_tensor_reduce(out=u_f[:, t * D:(t + 1) * D], in0=h_f[:, t * D:(t + 1) * D], in1=h_f[:, t * D:(t + 1) * D],
                                                scale=1.0, scalar=0.0, op0=ALU.mult, op1=ALU.add,
                                                accum_out=vec[5][:, t:t + 1])
            then(last)
            then(dve.tensor_scalar(vec[4], vec[5], 1e-20, None, ALU.max))
            dve.reciprocal(vec[0], vec[4]).then_inc(s_rvar, 1)
            dve.wait_ge(s_sqrt, 2)
            newton(vec, HS, s_step)
            for t in range(T):
                dve.tensor_scalar(u_f[:, t * D:(t + 1) * D], h_f[:, t * D:(t + 1) * D], vec[2][:, t:t + 1], None,
                                  ALU.mult).then_inc(s_unit, 1)
            for g in range(NS):
                dve.wait_ge(s_uhi, g + 1)
                dve.tensor_tensor(unit_t[:, N + g * ROWS:N + (g + 1) * ROWS], ps[:, 4 + g % 4, :],
                                  unit_t[:, g * ROWS:(g + 1) * ROWS], ALU.subtract).then_inc(s_ulo, 1)
            dve.wait_ge(s_cs, 1)
            then(dve.tensor_scalar(mean_h[:, :], ps[:, 0, 0:D], 1.0 / (HS * N), None, ALU.mult))
            then(dve.scalar_tensor_tensor(mean_h[:, :], ps[:, 0, D:2 * D], 1.0 / (HS * N), mean_h[:, :],
                                          ALU.mult, ALU.add))

            dve.sem_inc(s_adjm1, CREDIT)
            dve.sem_inc(s_pv, CREDIT)
            dve.sem_inc(s_adjt, CREDIT)
            dve.sem_inc(s_elo, CREDIT)
            dve.sem_inc(s_scores, 1)
            dve.sem_inc(s_evac, 1)
            dve.wait_ge(s_stage[0], 16)
            dve.tensor_scalar(adjm1b[:, 0:TPS * PW], stage[:, 0:TPS * PW], -FP8_MINUS_ONE, FP8_MINUS_ONE, ALU.mult, ALU.add).then_inc(s_adjm1, 1)
            with dve.Fori(0, NS) as s:
                with dve.Fori(0, PAIRS // UNROLL) as k:
                    m = s * PIECES + k * 2
                    for u in range(UNROLL):
                        if u == 0:
                            dve.wait_ge(s_stage[1], (s * (PIECES // 2) + k + 1) * 16)
                            dve.wait_ge(s_scores, m * 2 + 1)
                            dve.tensor_scalar(adjm1b[:, TPS * PW:], stage[:, TPS * PW:], -FP8_MINUS_ONE, FP8_MINUS_ONE, ALU.mult, ALU.add
                                              ).then_inc(s_adjm1, 1)
                        if u == 2:
                            with dve.If(s * (PAIRS // UNROLL) + k < NS * PAIRS // UNROLL - 1):
                                dve.wait_ge(s_stage[0], (s * (PIECES // 2) + k + 2) * 16)
                                dve.wait_ge(s_scores, m * 2 + 3)
                                dve.tensor_scalar(adjm1b[:, 0:TPS * PW], stage[:, 0:TPS * PW], -FP8_MINUS_ONE, FP8_MINUS_ONE, ALU.mult, ALU.add
                                                  ).then_inc(s_adjm1, 1)
                        n = s * PAIRS + k * UNROLL + u
                        bank = 4 + 2 * (u % 2)
                        sl = slice((u % 2) * 2 * ROWS, (u % 2 + 1) * 2 * ROWS)
                        dve.wait_ge(s_ehi, n + 1)
                        dve.tensor_scalar(adj_tb[:, bass.ds(s * T * ROWS + k * UNROLL * 2 * ROWS + u * 2 * ROWS, 2 * ROWS)],
                                          e_hi[:, sl], 0.0, FP8_ONE, ALU.is_gt, ALU.mult).then_inc(s_adjt, 1)
                        dve.wait_ge(s_exp, n + 1)
                        dve.wait_ge(s_pv, n + 1)
                        dve.tensor_tensor(e_lo[:, sl], ps[:, bank:bank + 2, :].rearrange("p a b -> p (a b)"),
                                          e_hi[:, sl], ALU.subtract).then_inc(s_elo, 1)
                EV = 5
                dve.wait_ge(s_pv, s * PAIRS + (PAIRS + CREDIT))
                dve.tensor_scalar(no_edge, ps[:, 0:TPS, 2 * D], 0.0, None, ALU.is_equal).then_inc(s_evs, 1)
                dve.wait_ge(s_evs, s * EV + 1)
                dve.scalar_tensor_tensor(den_s, ps[:, 0:TPS, 2 * D], HS, no_edge, ALU.mult, ALU.add).then_inc(s_evs, 1)
                dve.wait_ge(s_evs, s * EV + 2)
                dve.reciprocal(rden, den_s).then_inc(s_evs, 1)
                dve.wait_ge(s_evs, s * EV + 3)

                def rows(t):
                    return x_sb[:, bass.ds(s * ROWS + t * D, D)]

                for t in range(TPS):
                    last = dve.scalar_tensor_tensor(rows(t), ps[:, t, 0:D], rden[:, t:t + 1], rows(t),
                                                    ALU.mult, ALU.add)
                last.then_inc(s_evs, 1)
                dve.wait_ge(s_evs, s * EV + 4)
                for t in range(TPS):
                    last = dve.scalar_tensor_tensor(rows(t), ps[:, t, D:2 * D], rden[:, t:t + 1], rows(t),
                                                    ALU.mult, ALU.add)
                last.then_inc(s_evac, 1)
                dve.wait_ge(s_evac, s + 2)
                for t in range(TPS):
                    last = dve.scalar_tensor_tensor(rows(t), mean_h[:, :], no_edge[:, t:t + 1], rows(t),
                                                    ALU.mult, ALU.add)
                last.then_inc(s_evs, 1)
                dve.wait_ge(s_evs, s * EV + EV)

            steps[0] = 0
            dve.wait_ge(s_scores, NS * PAIRS + 1)
            row_scales(None, stats2, mv2, vec2, GS, s_step2, s_rvar2, s_sqrt2, 1, s_rstd2)
            tv = table[:, :].rearrange("p (t w) -> p t w", w=TW)
            xv = x_sb[:, :].rearrange("p (t d) -> p t d", d=D)
            for g in range(NS):
                a, b = g * TPS, (g + 1) * TPS
                gp = ps[:, 2 * (g % 2):2 * (g % 2) + 2, :].rearrange("p a (b c) -> p (a b) c", b=2)
                dve.wait_ge(s_ghi, g + 1)
                dve.wait_ge(s_h2, T)
                dve.scalar_tensor_tensor(xv[:, a:b, :], gp[:, :, D:2 * D], 1.0 / GS, xv[:, a:b, :], ALU.mult, ALU.add)
                dve.tensor_tensor(tv[:, a:b, 0:D], gp[:, :, 0:D], tv[:, a:b, D:2 * D], ALU.subtract
                                  ).then_inc(s_gtab, 1)
            dve.wait_ge(s_gtab, NS)
            for g in range(NS):
                b0 = 4 * (g % 2)
                dve.wait_ge(s_agg, g + 1)
                then(dve.tensor_scalar(den_s, ps[:, b0:b0 + 4, 2 * D], 1.0, GS, ALU.max, ALU.mult), s_step2)
                then(dve.reciprocal(rden, den_s), s_step2)
                for h in range(2):
                    for t in range(TPS):
                        r = x_sb[:, g * ROWS + t * D:g * ROWS + (t + 1) * D]
                        last = dve.scalar_tensor_tensor(r, ps[:, b0 + t, h * D:(h + 1) * D], rden[:, t:t + 1], r,
                                                        ALU.mult, ALU.add)
                    if h == 0:
                        then(last, s_step2)
                last.then_inc(s_res, 1)

        @block.tensor
        def _(pe):
            pe.wait_ge(s_ident, 2)
            for g in range(NS):
                pe.wait_ge(s_unit, (g + 1) * TPS)
                if g >= 4:
                    pe.wait_ge(s_ulo, g - 3)
                for t in range(TPS):
                    at = (g * TPS + t) * D
                    last = pe.transpose(ps[:, 4 + g % 4, t * P:(t + 1) * P], u_f[:, at:at + D], ident)
                last.then_inc(s_tp, 1)
            pe.wait_ge(s_first, 3)
            pe.wait_ge(s_tab, NS)
            for t in range(T):
                last = pe.matmul(ps[:, 0, 0:TW], ones_w, tab(t), start=(t == 0), stop=(t == T - 1))
            last.then_inc(s_cs, 1)
            pe.wait_ge(s_ulo, NS)
            pe.wait_ge(s_maskid, 1)

            def scores(s, pair, par, piece_par, n):
                pe.wait_ge(s_elo, n + 1)
                for c in range(2):
                    dst = ps[:, 4 + 2 * par + c, :]
                    ch = pair * (2 * P) + c * P
                    hi_j, lo_j = unit_t[:, bass.ds(ch, P)], unit_t[:, bass.ds(N + ch, P)]
                    hi_i, lo_i = unit_t[:, bass.ds(s * ROWS, ROWS)], unit_t[:, bass.ds(N + s * ROWS, ROWS)]
                    pe.matmul(dst, lo_j, hi_i, start=True, stop=False)
                    pe.matmul(dst, hi_j, lo_i, start=False, stop=False)
                    pe.matmul(dst, hi_j, hi_i, start=False, stop=False)
                    for t in range(TPS):
                        at = (piece_par * TPS + t) * PW + (2 * par + c) * P
                        last = pe.matmul(dst[:, t * P:(t + 1) * P], adjm1[:, at:at + P], mask_id[:, :],
                                         start=False, stop=(t == TPS - 1))
                last.then_inc(s_scores, 1)

            def attend(pair, par, n, end):
                for part, ready, lo in ((e_hi, s_ehi, 0), (e_lo, s_elo, D)):
                    pe.wait_ge(ready, n + (1 if part is e_hi else 1 + CREDIT))
                    for c in range(2):
                        mov = table[:, bass.ds((pair * 2 + c) * TW + lo, TW - lo)]
                        for t in range(TPS):
                            at = par * 2 * ROWS + c * ROWS + t * P
                            last = pe.matmul(ps[:, t, lo:TW], part[:, at:at + P], mov, start=False,
                                             stop=end and part is e_lo and c == 1)
                last.then_inc(s_pv, 1)

            with pe.Fori(0, NS) as s:
                pe.wait_ge(s_adjm1, s * PIECES + 1 + CREDIT)
                scores(s, 0, 0, 0, s * PAIRS)
                pe.wait_ge(s_evac, s + 1)
                for t in range(TPS):
                    pe.matmul(ps[:, t, 0:TW], zeros_w[:, :], tab(0), start=True, stop=False)

                def body(k, end):
                    for u in range(UNROLL):
                        n = s * PAIRS + k * UNROLL + u
                        if not (end and u == UNROLL - 1):
                            v = (u + 1) % UNROLL
                            if v % 2 == 0:
                                pe.wait_ge(s_adjm1, s * PIECES + k * 2 + (2 if v == 2 else 3) + CREDIT)
                            scores(s, k * UNROLL + (u + 1), v % 2, v // 2, n + 1)
                        attend(k * UNROLL + u, u % 2, n, end and u == UNROLL - 1)

                with pe.Fori(0, PAIRS // UNROLL - 1) as k:
                    body(k, False)
                body(PAIRS // UNROLL - 1, True)

            pe.wait_ge(s_ident2, 2)
            pe.wait_ge(s_w, 32)
            pe.wait_ge(s_evac, NS + 1)

            def transpose_h2(g):
                pe.wait_ge(s_h2, (g + 1) * TPS)
                if g >= 2:
                    pe.wait_ge(s_h2t, g - 1)
                for t in range(TPS):
                    at = (g * TPS + t) * D
                    last = pe.transpose(ps[:, 6 + g % 2, t * P:(t + 1) * P], h2_f[:, at:at + D], ident2)
                last.then_inc(s_h2p, 1)

            transpose_h2(0)
            for g in range(NS):
                if g + 1 < NS:
                    transpose_h2(g + 1)
                pe.wait_ge(s_h2t, g + 1)
                if g >= 2:
                    pe.wait_ge(s_gtab, g - 1)
                for t in range(TPS):
                    last = pe.matmul(ps[:, 2 * (g % 2) + t // 2, (t % 2) * 256:(t % 2 + 1) * 256],
                                     h2_t[g % 2][:, t * P:(t + 1) * P], w_cat, start=(t % 2 == 0), stop=True,
                                     skip_group_check=True)
                last.then_inc(s_g, 1)
            pe.wait_ge(s_gtab, NS)
            pe.wait_ge(s_adjt, NS * PAIRS + CREDIT)
            for g in range(NS):
                if g >= 2:
                    pe.wait_ge(s_res, g - 1)
                for b in range(T):
                    for t in range(TPS):
                        at = (g * T + b) * ROWS + t * P
                        last = pe.matmul(ps[:, 4 * (g % 2) + t, 0:TW], adj_t[:, at:at + P], tab(b),
                                         start=(b == 0), stop=(b == T - 1))
                last.then_inc(s_agg, 1)


_INS = ["x", "adj", "L0_gnn_beta", "L1_gnn_W_self", "L1_gnn_W_neigh"]


def kernel(**inputs):
    import numpy as _np
    import concourse.bacc as _bacc
    from concourse import mybir as _mybir
    from concourse.bass_utils import run_bass_kernel_spmd as _run

    nc = _bacc.Bacc("TRN2", target_bir_lowering=False, num_devices=1)
    arrays, args = {}, []
    for name in _INS:
        a = _np.ascontiguousarray(inputs[name])
        arrays[f"in_{name}_dram"] = a
        args.append(nc.dram_tensor(f"in_{name}_dram", a.shape, _mybir.dt.from_np(a.dtype), kind="ExternalInput").ap())
    shape = inputs["x"].shape
    args.append(nc.dram_tensor("out_0_dram", shape, _mybir.dt.float32, kind="ExternalOutput").ap())
    gnn_program(nc, *args)
    r = _run(nc, [arrays], core_ids=[0])
    return r.results[0]["out_0_dram"]
```

```python
import concourse.bass as bass
from concourse import mybir
from contextlib import ExitStack


def gnn_program(nc, x_in, adj_in, beta_in, w_self_in, w_neigh_in, out):
    fp32, fp16, bf16, fp8 = mybir.dt.float32, mybir.dt.float16, mybir.dt.bfloat16, mybir.dt.float8e4
    u8 = mybir.dt.uint8
    ALU, ACT = mybir.AluOpType, mybir.ActivationFunctionType

    N, D = x_in.shape
    P = 128
    T = N // P
    ROWS = 512
    TPS = ROWS // P
    NS = N // ROWS
    PAIRS = T // 2
    PIECES = PAIRS // 2
    PW = 4 * P
    UNROLL = 4
    HS = 256.0
    CREDIT_ADJ = 3
    E_BITS = 14
    LN2 = 0.6931471805599453
    MASK = 2.0 ** 30
    EPS = 1e-5
    FP8_ONE, FP8_MINUS_ONE = 0x38, 0xB8
    TW = 2 * D + 1

    x_v = x_in.rearrange("(t p) d -> p t d", p=P)
    out_v = out.rearrange("(t p) d -> p t d", p=P)
    adj_v = adj_in.rearrange("(t p) j -> p t j", p=P)

    ctx = ExitStack()
    with ctx:
        def sb(name, shape, dt):
            return ctx.enter_context(nc.sbuf_tensor(name, shape, dt))

        def sem(name):
            return ctx.enter_context(nc.semaphore(name))

        adj_tb = sb("adj_t", [P, NS * T * ROWS], u8)
        x_sb = sb("x_sb", [P, T * D], fp32)
        table = sb("table", [P, T * TW], fp16)
        unit_t = sb("unit_t", [P, 2 * N], fp16)
        stage = sb("stage", [P, 2 * TPS * PW], fp32)
        adjm1b = sb("adjm1", [P, 2 * TPS * 2 * P], u8)
        e_hi = sb("e_hi", [P, 2 * 2 * ROWS], fp16)
        e_lo = sb("e_lo", [P, 2 * 2 * ROWS], fp16)
        acc_sb = sb("acc_sb", [P, TPS * TW], fp32)
        small = sb("small", [P, 48], fp32)
        scales2 = sb("scales2", [P, 2 * T], fp32)
        mask_id = sb("mask_id", [P, P], bf16)
        mean_h = sb("mean_h", [P, D], fp32)
        zeros_w = sb("zeros_w", [P, P], fp16)
        ps = ctx.enter_context(nc.psum_tensor("ps", [P, 8, 512], fp32))

        adj_t = adj_tb[:, :].bitcast(fp8)
        adjm1 = adjm1b[:, :].bitcast(fp8)

        room = [0]

        def early(count, dt):
            size = count * (2 if dt == fp16 else 4)
            ap = adj_t[:, room[0]:room[0] + size].bitcast(dt)
            room[0] += size
            return ap

        h_f = early(T * D, fp32)
        u_f = early(T * D, fp32)
        stats = early(T * 6, fp32)
        mv = early(T * 2, fp32)
        ident = early(P, fp32)
        ones_w = early(P, fp16)
        var_e, rstd, scale_h, bias_h, norm2, norm2_g, rnorm = [early(T, fp32) for _ in range(7)]
        neg_half = small[:, 32:40]
        c_scale = small[:, 40:44]
        c_minus = small[:, 44:48]

        h2_f = unit_t[:, :].bitcast(fp32)
        w_cat = stage[:, 0:2 * D]
        ident2 = stage[:, 256:384]
        neigh = stage[:, 512:1024]
        neigh_t = stage[:, 1024:1536]
        h2_t = stage[:, 1536:2048]

        beta = small[:, 0:1]
        beta_s = small[:, 1:2]
        exp_scale = small[:, 2:3]
        exp_bias = small[:, 3:4]
        b_sq = small[:, 4:5]
        b_zero = small[:, 5:6]
        b_inv = small[:, 6:7]
        b_keep = small[:, 7:8]
        b_pos = small[:, 8:9]
        no_edge = small[:, 12:16]
        den_s = small[:, 16:20]
        rden = small[:, 20:24]
        stats2 = small[:, 24:30]
        mv2 = small[:, 30:32]
        mean2 = scales2[:, 0:T]
        var2 = scales2[:, T:2 * T]

        def tab(t, lo=0, hi=TW):
            return table[:, t * TW + lo:t * TW + hi]

        tab_v = table[:, :].rearrange("p (t w) -> p t w", w=TW)
        acc_v = acc_sb[:, :].rearrange("p (t w) -> p t w", w=TW)

        XP = 4
        TX = T // XP
        s_x = [sem(f"x_loaded{i}") for i in range(XP)]
        s_beta = sem("beta_loaded")
        s_w = sem("weights_loaded")
        s_stage = [sem(f"stage_loaded{i}") for i in range(2)]
        s_out = sem("out_stored")
        s_ident = sem("ident_ready")
        s_first = sem("constants_ready")
        s_maskid = sem("mask_identity_ready")
        s_step = sem("dve_step")
        s_var = sem("variance_ready")
        s_rstd = sem("rstd_ready")
        s_scales = sem("scales_ready")
        s_h = sem("h_ready")
        s_norm2 = sem("norm2_ready")
        s_rnorm = sem("rnorm_ready")
        s_unit = sem("unit_ready")
        s_tp = sem("transposed")
        s_uhi = sem("unit_hi_ready")
        s_ulo = sem("unit_lo_ready")
        s_hh = sem("table_high_ready")
        s_tab = sem("table_ready")
        s_cs = sem("colsum_ready")
        s_adjm1 = sem("adjm1_ready")
        s_scores = sem("scores_ready")
        s_ehi = sem("exp_hi_ready")
        s_exp = sem("exp_ready")
        s_elo = sem("exp_lo_ready")
        s_adjt = sem("adj_t_ready")
        s_pvhi = sem("pv_high_done")
        s_pvlo = sem("pv_low_done")
        s_evac = sem("acc_evacuated")
        s_den = sem("denominator_step")
        s_rows = sem("rows_step")
        s_pool_waited = sem("pool_waited")
        s_dve_waited = sem("dve_waited")
        s_var2 = sem("variance2_ready")
        s_pool2 = sem("pool_step2")
        s_rs2 = sem("scales2_ready")
        s_h2 = sem("h2_ready")
        s_hh2 = sem("table2_high_ready")
        s_tab2 = sem("table2_ready")
        s_ident2 = sem("ident2_ready")
        s_agg = sem("agg_ready")
        s_aggden = sem("agg_step")
        s_neigh = sem("neigh_ready")
        s_post_t = sem("post_transposed")
        s_post_c = sem("post_copied")
        s_post_m = sem("post_multiplied")
        s_res = sem("result_ready")
        RS = 8
        CREDIT = 2
        ONE = 1

        block = ctx.enter_context(nc.Block())

        @block.sync
        def _(sp):
            for i in range(XP):
                sp.dma_start(x_sb[:, i * TX * D:(i + 1) * TX * D].rearrange("p (t d) -> p t d", d=D),
                             x_v[:, TX * i:TX * (i + 1), :]).then_inc(s_x[i], 16)
                if i == 0:
                    sp.dma_start(beta, beta_in.partition_broadcast(P)).then_inc(s_beta, 16)
            with sp.Fori(0, NS) as s:
                with sp.Fori(0, PIECES // 2) as q:
                    for i in range(2):
                        sp.wait_ge(s_adjm1, s * PAIRS + q * 4 + (2 * i - 4 + 2 + CREDIT_ADJ))
                        sp.dma_start(stage[:, i * TPS * PW:(i + 1) * TPS * PW].rearrange("p (t c) -> p t c", c=PW),
                                     adj_v[:, bass.ds(s * TPS, TPS), bass.ds(q * 2 * PW + i * PW, PW)]
                                     ).then_inc(s_stage[i], 16)
            sp.wait_ge(s_adjm1, NS * PAIRS + CREDIT_ADJ)
            sp.dma_start(w_cat[:, 0:D], w_neigh_in).then_inc(s_w, 16)
            sp.dma_start(w_cat[:, D:2 * D], w_self_in).then_inc(s_w, 16)
            for g in range(NS):
                sp.wait_ge(s_res, g + 1)
                sp.dma_start(out_v[:, g * TPS:(g + 1) * TPS, :],
                             x_sb[:, g * ROWS:(g + 1) * ROWS].rearrange("p (t d) -> p t d", d=D)).then_inc(s_out, 16)
            sp.wait_ge(s_out, 16 * NS)

        @block.gpsimd
        def _(pool):
            pool.memset(c_scale, HS).then_inc(s_first, 1)
            pool.memset(c_minus, -1.0).then_inc(s_first, 1)
            pool.memset(neg_half, -0.5).then_inc(s_first, 1)
            pool.memset(ident, 0.0).then_inc(s_ident, 1)
            pool.memset(ones_w, 1.0).then_inc(s_first, 1)
            pool.memset(zeros_w[:, :], 0.0).then_inc(s_first, 1)
            pool.memset(tab_v[:, :, 2 * D:TW], 1.0).then_inc(s_first, 1)
            pool.wait_ge(s_ident, 1)
            pool.affine_select(out=ident, in_=ident, compare_op=ALU.not_equal, fill=1.0, base=0,
                               pattern=[[-1, P]], channel_multiplier=1).then_inc(s_ident, 1)
            pool.wait_ge(s_first, 3)
            hv = h_f.rearrange("p (t d) -> p t d", d=D)

            def low_parts(g):
                a, b = g * TPS, (g + 1) * TPS
                pool.wait_ge(s_hh, g + 1)
                pool.tensor_tensor(tab_v[:, a:b, 0:D], hv[:, a:b, :], tab_v[:, a:b, D:2 * D], ALU.subtract
                                   ).then_inc(s_tab, 1)

            for i in range(XP + 1):
                if i < XP:
                    part = slice(i * TX, (i + 1) * TX)
                    pool.wait_ge(s_var, i + 1)
                    pool.tensor_tensor(rstd[:, part], var_e[:, part], neg_half, ALU.pow).then_inc(s_rstd, 1)
                if i >= 1:
                    part = slice((i - 1) * TX, i * TX)
                    pool.wait_ge(s_norm2, i)
                    pool.tensor_tensor(rnorm[:, part], norm2_g[:, part], neg_half, ALU.pow).then_inc(s_rnorm, 1)
            for g in range(NS):
                low_parts(g)

            def convert(u):
                slot, half = u // 2, u % 2
                src = stage[:, slot * TPS * PW:(slot + 1) * TPS * PW].rearrange("p (t c) -> p t c", c=PW)
                dst = adjm1b[:, half * TPS * 2 * P:(half + 1) * TPS * 2 * P].rearrange("p (t c) -> p t c", c=2 * P)
                pool.tensor_scalar(dst, src[:, :, half * 2 * P:(half + 1) * 2 * P], -FP8_MINUS_ONE, FP8_MINUS_ONE,
                                   ALU.mult, ALU.add).then_inc(s_adjm1, 1)

            def scales_of_x2(s):
                var, mean = var2[:, s * TPS:(s + 1) * TPS], mean2[:, s * TPS:(s + 1) * TPS]
                at = s * 3
                pool.wait_ge(s_var2, (s + 1) * TPS)
                pool.tensor_tensor(var, var, neg_half[:, 0:TPS], ALU.pow).then_inc(s_pool2, 1)
                pool.wait_ge(s_pool2, at + 1)
                pool.tensor_tensor(var, var, c_scale, ALU.mult).then_inc(s_pool2, 1)
                pool.wait_ge(s_pool2, at + 2)
                pool.tensor_tensor(mean, mean, var, ALU.mult).then_inc(s_pool2, 1)
                pool.wait_ge(s_pool2, at + 3)
                pool.tensor_tensor(mean, mean, c_minus, ALU.mult).then_inc(s_rs2, 1)

            for s in range(NS):
                with pool.Fori(0, PAIRS // UNROLL) as k:
                    for u in range(UNROLL):
                        if u % 2 == 0:
                            pool.wait_ge(s_stage[u // 2], (k + (s * (PIECES // 2) + 1)) * 16)
                        pool.wait_ge(s_scores, k * UNROLL + (s * PAIRS + u - 1 + CREDIT))
                        pool.sem_inc(s_pool_waited, 1)
                        convert(u)
                if s >= 2:
                    scales_of_x2(s - 2)
            scales_of_x2(NS - 2)
            pool.wait_ge(s_adjm1, NS * PAIRS + CREDIT_ADJ)
            pool.memset(ident2, 0.0).then_inc(s_ident2, 1)
            pool.wait_ge(s_ident2, 1)
            pool.affine_select(out=ident2, in_=ident2, compare_op=ALU.not_equal, fill=1.0, base=0,
                               pattern=[[-1, P]], channel_multiplier=1).then_inc(s_ident2, 1)
            scales_of_x2(NS - 1)

        @block.scalar
        def _(act):
            act.preload_act_table(ACT.Exp)

            def unit_high(g):
                act.wait_ge(s_tp, g + 1)
                act.activation(unit_t[:, g * ROWS:(g + 1) * ROWS], ps[:, 4 + g % 4, :], ACT.Copy).then_inc(s_uhi, 1)

            for i in range(XP):
                act.wait_ge(s_scales, i + 1)
                for t in range(i * TX, (i + 1) * TX):
                    act.activation(h_f[:, t * D:(t + 1) * D], x_sb[:, t * D:(t + 1) * D], ACT.Relu,
                                   bias=bias_h[:, t:t + 1], scale=scale_h[:, t:t + 1]).then_inc(s_h, 1)
                    if t % TPS == TPS - 1:
                        a, b = t - TPS + 1, t + 1
                        act.wait_ge(s_h, t + 1)
                        act.activation(tab_v[:, a:b, D:2 * D], h_f.rearrange("p (t d) -> p t d", d=D)[:, a:b, :],
                                       ACT.Copy).then_inc(s_hh, 1)
                if i >= 1:
                    unit_high(2 * i - 2)
                    unit_high(2 * i - 1)
            unit_high(NS - 2)
            unit_high(NS - 1)

            with act.Fori(0, NS) as s:
                with act.Fori(0, PAIRS // UNROLL) as k:
                    for u in range(UNROLL):
                        n = s * PAIRS + k * UNROLL + u
                        bank = 4 + 2 * (u % 2)
                        hi = e_hi[:, (u % 2) * 2 * ROWS:(u % 2 + 1) * 2 * ROWS]
                        sc = ps[:, bank:bank + 2, :].rearrange("p a b -> p (a b)")
                        act.wait_ge(s_scores, n + 1 + CREDIT)
                        act.wait_ge(s_pvhi, n - 1 + CREDIT)
                        act.wait_ge(s_adjt, n - 1 + CREDIT)
                        act.activation(hi, sc, ACT.Exp, bias=exp_bias, scale=exp_scale).then_inc(s_ehi, 1)
                        act.activation(sc, sc, ACT.Exp, bias=exp_bias, scale=exp_scale).then_inc(s_exp, 1)

            for t in range(T):
                if t % TPS == 0:
                    act.wait_ge(s_rs2, t // TPS + 1)
                act.activation(h2_f[:, t * D:(t + 1) * D], x_sb[:, t * D:(t + 1) * D], ACT.Relu,
                               bias=mean2[:, t:t + 1], scale=var2[:, t:t + 1]).then_inc(s_h2, 1)
            for g in range(NS):
                b0 = 4 * (g % 2)
                act.wait_ge(s_post_t, g + 1)
                if g >= 1:
                    act.wait_ge(s_post_m, g)
                act.activation(neigh_t, ps[:, b0, :], ACT.Copy).then_inc(s_post_c, 1)
                act.activation(h2_t, ps[:, b0 + 1, :], ACT.Copy, scale=1.0 / HS).then_inc(s_post_c, 1)

        @block.vector
        def _(dve):
            steps = [0]

            def then(ins):
                steps[0] += 1
                ins.then_inc(s_step, 1)
                dve.wait_ge(s_step, steps[0])

            mv_v = mv.rearrange("p (t c) -> p t c", c=2)

            def variances(i):
                dve.wait_ge(s_x[i], 16)
                for t in range(i * TX, (i + 1) * TX):
                    last = dve.bn_stats(stats[:, t * 6:(t + 1) * 6], x_sb[:, t * D:(t + 1) * D])
                then(last)
                for t in range(i * TX, (i + 1) * TX):
                    last = dve.bn_aggr(mv[:, t * 2:(t + 1) * 2], stats[:, t * 6:(t + 1) * 6])
                then(last)
                dve.tensor_scalar(var_e[:, i * TX:(i + 1) * TX], mv_v[:, i * TX:(i + 1) * TX, 1], EPS, None,
                                  ALU.add).then_inc(s_var, 1)

            def scales(i):
                part = slice(i * TX, (i + 1) * TX)
                dve.wait_ge(s_rstd, i + 1)
                then(dve.tensor_scalar(scale_h[:, part], rstd[:, part], HS, None, ALU.mult))
                dve.scalar_tensor_tensor(bias_h[:, part], mv_v[:, part, 0], -1.0, scale_h[:, part],
                                         ALU.mult, ALU.mult).then_inc(s_scales, 1)

            def norms(i):
                part = slice(i * TX, (i + 1) * TX)
                for t in range(i * TX, (i + 1) * TX):
                    dve.wait_ge(s_h, t + 1)
                    last = dve.tensor_tensor_reduce(
                        out=u_f[:, t * D:(t + 1) * D], in0=h_f[:, t * D:(t + 1) * D], in1=h_f[:, t * D:(t + 1) * D],
                        scale=1.0, scalar=0.0, op0=ALU.mult, op1=ALU.add, accum_out=norm2[:, t:t + 1])
                then(last)
                dve.tensor_scalar(norm2_g[:, part], norm2[:, part], 1e-20, None, ALU.max).then_inc(s_norm2, 1)

            def units(i):
                dve.wait_ge(s_rnorm, i + 1)
                for t in range(i * TX, (i + 1) * TX):
                    dve.tensor_scalar(u_f[:, t * D:(t + 1) * D], h_f[:, t * D:(t + 1) * D], rnorm[:, t:t + 1], HS,
                                      ALU.mult, ALU.mult).then_inc(s_unit, 1)

            def unit_low(g):
                dve.wait_ge(s_uhi, g + 1)
                dve.tensor_tensor(unit_t[:, N + g * ROWS:N + (g + 1) * ROWS], ps[:, 4 + g % 4, :],
                                  unit_t[:, g * ROWS:(g + 1) * ROWS], ALU.subtract).then_inc(s_ulo, 1)

            dve.sem_inc(s_adjm1, CREDIT_ADJ)
            dve.sem_inc(s_pvhi, CREDIT)
            dve.sem_inc(s_pvlo, CREDIT)
            dve.sem_inc(s_adjt, CREDIT)
            dve.sem_inc(s_elo, CREDIT)
            dve.sem_inc(s_scores, CREDIT)
            dve.sem_inc(s_rows, TPS * RS)
            variances(0)
            scales(0)
            variances(1)
            scales(1)
            dve.wait_ge(s_beta, 16)
            then(dve.tensor_tensor(b_sq, beta, beta, ALU.mult))
            then(dve.tensor_scalar(b_zero, b_sq, 1e-36, 1e-18, ALU.is_le, ALU.mult))
            then(dve.tensor_scalar(b_keep, b_sq, 1e-36, None, ALU.is_gt))
            then(dve.scalar_tensor_tensor(beta_s, beta, b_keep, b_zero, ALU.mult, ALU.add))
            then(dve.reciprocal(b_inv, beta_s))
            then(dve.tensor_scalar(exp_scale, beta_s, 1.0 / (HS * HS), None, ALU.mult))
            then(dve.tensor_scalar(b_pos, beta, 0.0, None, ALU.max))
            then(dve.tensor_scalar(exp_bias, b_pos, -1.0, E_BITS * LN2, ALU.mult, ALU.add))
            dve.wait_ge(s_ident, 2)
            dve.tensor_scalar(mask_id[:, :], ident, b_inv, MASK * HS * HS, ALU.mult, ALU.mult).then_inc(s_maskid, 1)
            norms(0)
            variances(2)
            scales(2)
            units(0)
            norms(1)
            variances(3)
            scales(3)
            units(1)
            unit_low(0)
            unit_low(1)
            norms(2)
            unit_low(2)
            unit_low(3)
            units(2)
            norms(3)
            unit_low(4)
            unit_low(5)
            units(3)
            unit_low(6)
            unit_low(7)

            dve.wait_ge(s_cs, 1)
            then(dve.tensor_scalar(mean_h[:, :], ps[:, 0, 0:D], 1.0 / (HS * N), None, ALU.mult))
            dve.scalar_tensor_tensor(mean_h[:, :], ps[:, 0, D:2 * D], 1.0 / (HS * N), mean_h[:, :],
                                     ALU.mult, ALU.add).then_inc(s_evac, ONE)


            def finish_rows(step, done, x_row, acc, at, mean_dst, var_dst):
                def after(i):
                    dve.wait_ge(s_rows, at + i)

                ne, den, r = no_edge[:, 0:1], den_s[:, 0:1], rden[:, 0:1]
                if step == 0:
                    dve.wait_ge(s_evac, done + ONE)
                    dve.tensor_scalar(ne, acc(2 * D, 1), 0.0, None, ALU.is_equal).then_inc(s_rows, 1)
                    after(1)
                    dve.scalar_tensor_tensor(den, acc(2 * D, 1), HS, ne, ALU.mult, ALU.add).then_inc(s_rows, 1)
                    after(2)
                    dve.reciprocal(r, den).then_inc(s_rows, 1)
                if step == 1:
                    after(3)
                    dve.scalar_tensor_tensor(x_row, acc(0, D), r, x_row, ALU.mult, ALU.add).then_inc(s_rows, 1)
                if step == 2:
                    after(4)
                    dve.scalar_tensor_tensor(x_row, acc(D, D), r, x_row, ALU.mult, ALU.add).then_inc(s_rows, 1)
                    after(5)
                    dve.scalar_tensor_tensor(x_row, mean_h[:, :], ne, x_row, ALU.mult, ALU.add).then_inc(s_rows, 1)
                if step == 3:
                    after(6)
                    dve.bn_stats(stats2, x_row).then_inc(s_rows, 1)
                    after(7)
                    dve.sem_inc(s_dve_waited, 1)
                    dve.bn_aggr(mv2, stats2).then_inc(s_rows, 1)
                    after(8)
                    dve.tensor_copy(mean_dst, mv2[:, 0:1])
                    dve.tensor_scalar(var_dst, mv2[:, 1:2], EPS, None, ALU.add).then_inc(s_var2, 1)

            with dve.Fori(0, NS) as s:
                with dve.Fori(0, PAIRS // UNROLL) as k:
                    for u in range(UNROLL):
                        n = s * PAIRS + k * UNROLL + u
                        bank = 4 + 2 * (u % 2)
                        sl = slice((u % 2) * 2 * ROWS, (u % 2 + 1) * 2 * ROWS)
                        dve.wait_ge(s_ehi, n + 1)
                        dve.tensor_scalar(adj_tb[:, bass.ds(s * T * ROWS + k * UNROLL * 2 * ROWS + u * 2 * ROWS, 2 * ROWS)],
                                          e_hi[:, sl], 0.0, FP8_ONE, ALU.is_gt, ALU.mult).then_inc(s_adjt, 1)
                        dve.wait_ge(s_exp, n + 1)
                        dve.wait_ge(s_pvlo, n - 1 + CREDIT)
                        dve.tensor_tensor(e_lo[:, sl], ps[:, bank:bank + 2, :].rearrange("p a b -> p (a b)"),
                                          e_hi[:, sl], ALU.subtract).then_inc(s_elo, 1)
                        with dve.If(s > 0):
                            prev = nc.s_assert_within(s - 1, 0, NS - 2, 
                                skip_runtime_bounds_check_because="the branch is taken from the second supertile on")
                            finish_rows(u, s, x_sb[:, bass.ds(prev * ROWS + k * D, D)],
                                        lambda at, size: acc_sb[:, bass.ds(k * TW + at, size)],
                                        (s * TPS + k) * RS, mean2[:, bass.ds(prev * TPS + k, 1)],
                                        var2[:, bass.ds(prev * TPS + k, 1)])
                dve.wait_ge(s_pvlo, s * PAIRS + (PAIRS + CREDIT))
                dve.tensor_copy(acc_v, ps[:, 0:TPS, 0:TW]).then_inc(s_evac, 1)
            h2_v = h2_f.rearrange("p (t d) -> p t d", d=D)

            def second_table(g):
                a, b = g * TPS, (g + 1) * TPS
                dve.wait_ge(s_h2, (g + 1) * TPS)
                dve.tensor_copy(tab_v[:, a:b, D:2 * D], h2_v[:, a:b, :]).then_inc(s_hh2, 1)
                dve.wait_ge(s_hh2, g + 1)
                dve.tensor_tensor(tab_v[:, a:b, 0:D], h2_v[:, a:b, :], tab_v[:, a:b, D:2 * D], ALU.subtract
                                  ).then_inc(s_tab2, 1)

            second_table(0)
            for t in range(TPS):
                for u in range(UNROLL):
                    tn = T - TPS + t
                    finish_rows(u, NS, x_sb[:, tn * D:(tn + 1) * D],
                                lambda at, size: acc_sb[:, t * TW + at:t * TW + at + size],
                                (NS * TPS + t) * RS, mean2[:, tn:tn + 1], var2[:, tn:tn + 1])
            for g in range(1, NS):
                second_table(g)
            xg = x_sb[:, :].rearrange("p (g r) -> p g r", r=ROWS)
            for g in range(NS):
                b0 = 4 * (g % 2)
                dve.wait_ge(s_agg, g + 1)
                then(dve.tensor_scalar(den_s, ps[:, b0:b0 + 4, 2 * D], 1.0, HS, ALU.max, ALU.mult))
                then(dve.reciprocal(rden, den_s))
                for t in range(TPS):
                    last = dve.tensor_scalar(neigh[:, t * D:(t + 1) * D], ps[:, b0 + t, 0:D], rden[:, t:t + 1], None,
                                             ALU.mult)
                then(last)
                for t in range(TPS):
                    last = dve.scalar_tensor_tensor(neigh[:, t * D:(t + 1) * D], ps[:, b0 + t, D:2 * D],
                                                    rden[:, t:t + 1], neigh[:, t * D:(t + 1) * D], ALU.mult, ALU.add)
                last.then_inc(s_neigh, 1)
                dve.wait_ge(s_post_m, g + 1)
                dve.tensor_tensor(xg[:, g, :], ps[:, b0 + 2, :], xg[:, g, :], ALU.add).then_inc(s_res, 1)

        @block.tensor
        def _(pe):
            pe.wait_ge(s_ident, 2)
            for g in range(NS):
                pe.wait_ge(s_unit, (g + 1) * TPS)
                if g >= 4:
                    pe.wait_ge(s_ulo, g - 3)
                for t in range(TPS):
                    at = (g * TPS + t) * D
                    last = pe.transpose(ps[:, 4 + g % 4, t * P:(t + 1) * P], u_f[:, at:at + D], ident)
                last.then_inc(s_tp, 1)
            pe.wait_ge(s_ulo, NS)
            pe.wait_ge(s_maskid, 1)

            def scores(s, pair, par, n):
                pe.wait_ge(s_elo, n - 1 + CREDIT)
                pe.wait_ge(s_adjm1, n + 1 + CREDIT_ADJ)
                for c in range(2):
                    dst = ps[:, 4 + 2 * par + c, :]
                    ch = pair * (2 * P) + c * P
                    hi_j, lo_j = unit_t[:, bass.ds(ch, P)], unit_t[:, bass.ds(N + ch, P)]
                    hi_i, lo_i = unit_t[:, bass.ds(s * ROWS, ROWS)], unit_t[:, bass.ds(N + s * ROWS, ROWS)]
                    pe.matmul(dst, lo_j, hi_i, start=True, stop=False)
                    pe.matmul(dst, hi_j, lo_i, start=False, stop=False)
                    pe.matmul(dst, hi_j, hi_i, start=False, stop=False)
                    for t in range(TPS):
                        at = (par * TPS + t) * 2 * P + c * P
                        last = pe.matmul(dst[:, t * P:(t + 1) * P], adjm1[:, at:at + P], mask_id[:, :],
                                         start=False, stop=(t == TPS - 1))
                last.then_inc(s_scores, 1)

            def attend(part, pair, par, n, end=False):
                high = part is e_hi
                lo = 0 if high else D
                if high:
                    pe.wait_ge(s_ehi, n + 1)
                else:
                    pe.wait_ge(s_elo, n + 1 + CREDIT)
                for c in range(2):
                    mov = table[:, bass.ds((pair * 2 + c) * TW + lo, TW - lo)]
                    for t in range(TPS):
                        at = par * 2 * ROWS + c * ROWS + t * P
                        last = pe.matmul(ps[:, t, lo:TW], part[:, at:at + P], mov, start=False, stop=end and c == 1)
                last.then_inc(s_pvhi if high else s_pvlo, 1)

            scores(0, 0, 0, 0)
            pe.wait_ge(s_first, 6)
            pe.wait_ge(s_tab, NS)
            for t in range(T):
                last = pe.matmul(ps[:, 0, 0:TW], ones_w, tab(t), start=(t == 0), stop=(t == T - 1))
            last.then_inc(s_cs, 1)

            with pe.Fori(0, NS) as s:
                def body(k, first, end):
                    for u in range(UNROLL):
                        n = s * PAIRS + k * UNROLL + u
                        if not (end and u == UNROLL - 1):
                            scores(s, k * UNROLL + (u + 1), (u + 1) % 2, n + 1)
                        else:
                            with pe.If(s < NS - 1):
                                scores(nc.s_assert_within(s + 1, 1, NS - 1, skip_runtime_bounds_check_because=
                                    "the branch is not taken in the last supertile"), 0, 0, n + 1)
                        if first and u == 0:
                            pe.wait_ge(s_evac, s + ONE)
                            for t in range(TPS):
                                pe.matmul(ps[:, t, 0:TW], zeros_w[:, :], tab(0), start=True, stop=False)
                        attend(e_hi, k * UNROLL + u, u % 2, n)
                        if not (first and u == 0):
                            attend(e_lo, k * UNROLL + (u - 1), (u - 1) % 2, n - 1)
                    if end:
                        attend(e_lo, PAIRS - 1, (PAIRS - 1) % 2, n, end=True)

                body(0, True, False)
                with pe.Fori(1, PAIRS // UNROLL - 1) as k:
                    body(k, False, False)
                body(PAIRS // UNROLL - 1, False, True)

            def post_transpose(g):
                pe.wait_ge(s_neigh, g + 1)
                for src, bank in ((neigh, 0), (h2_f[:, g * ROWS:(g + 1) * ROWS], 1)):
                    for t in range(TPS):
                        last = pe.transpose(ps[:, 4 * (g % 2) + bank, t * P:(t + 1) * P], src[:, t * D:(t + 1) * D], ident2)
                last.then_inc(s_post_t, 1)

            def post_multiply(g):
                pe.wait_ge(s_post_c, 2 * g + 2)
                for t in range(TPS):
                    dst = ps[:, 4 * (g % 2) + 2, t * P:(t + 1) * P]
                    pe.matmul(dst, neigh_t[:, t * P:(t + 1) * P], w_cat[:, 0:D], start=True, stop=False)
                    last = pe.matmul(dst, h2_t[:, t * P:(t + 1) * P], w_cat[:, D:2 * D], start=False, stop=True)
                last.then_inc(s_post_m, 1)

            pe.wait_ge(s_evac, NS + ONE)
            pe.wait_ge(s_adjt, NS * PAIRS + CREDIT)
            for g in range(NS):
                if g >= 2:
                    pe.wait_ge(s_res, g - 1)
                for b in range(T):
                    if g == 0 and b % TPS == 0:
                        pe.wait_ge(s_tab2, b // TPS + 1)
                    for t in range(TPS):
                        at = (g * T + b) * ROWS + t * P
                        last = pe.matmul(ps[:, 4 * (g % 2) + t, 0:TW], adj_t[:, at:at + P], tab(b),
                                         start=(b == 0), stop=(b == T - 1))
                    if g >= 1 and b == T // 4:
                        if g == 1:
                            pe.wait_ge(s_ident2, 2)
                            pe.wait_ge(s_w, 32)
                        post_transpose(g - 1)
                    if g >= 1 and b == T // 2:
                        post_multiply(g - 1)
                last.then_inc(s_agg, 1)
            post_transpose(NS - 1)
            post_multiply(NS - 1)


_INS = ["x", "adj", "L0_gnn_beta", "L1_gnn_W_self", "L1_gnn_W_neigh"]


def kernel(**inputs):
    import numpy as _np
    import concourse.bacc as _bacc
    from concourse import mybir as _mybir
    from concourse.bass_utils import run_bass_kernel_spmd as _run

    nc = _bacc.Bacc("TRN2", target_bir_lowering=False, num_devices=1)
    arrays, args = {}, []
    for name in _INS:
        a = _np.ascontiguousarray(inputs[name])
        arrays[f"in_{name}_dram"] = a
        args.append(nc.dram_tensor(f"in_{name}_dram", a.shape, _mybir.dt.from_np(a.dtype), kind="ExternalInput").ap())
    shape = inputs["x"].shape
    args.append(nc.dram_tensor("out_0_dram", shape, _mybir.dt.float32, kind="ExternalOutput").ap())
    gnn_program(nc, *args)
    r = _run(nc, [arrays], core_ids=[0])
    return r.results[0]["out_0_dram"]
```

```python
import concourse.bass as bass
from concourse import mybir
from contextlib import ExitStack


def gnn_program(nc, x_in, adj_in, beta_in, w_self_in, w_neigh_in, out):
    fp32, fp16, bf16, fp8 = mybir.dt.float32, mybir.dt.float16, mybir.dt.bfloat16, mybir.dt.float8e4
    u8 = mybir.dt.uint8
    ALU, ACT = mybir.AluOpType, mybir.ActivationFunctionType

    N, D = x_in.shape
    P = 128
    T = N // P
    ROWS = 512
    TPS = ROWS // P
    NS = N // ROWS
    PAIRS = T // 2
    PIECES = PAIRS // 2
    PW = 4 * P
    UNROLL = 4
    WS = 32.0
    HS = 256.0
    CREDIT_ADJ = 3
    E_BITS = 14
    LN2 = 0.6931471805599453
    MASK = 2.0 ** 30
    EPS = 1e-5
    EPS_COS = 1e-7
    INV_PLAIN = 2.01 ** -0.5
    FACTOR_MAX = 2.0 ** 23
    FP8_ONE, FP8_MINUS_ONE = 0x38, 0xB8
    TW = 2 * D + 1

    XP = 4
    TX = T // XP

    x_v = x_in.rearrange("(t p) d -> p t d", p=P)
    out_v = out.rearrange("(t p) d -> p t d", p=P)
    adj_v = adj_in.rearrange("(t p) j -> p t j", p=P)

    inv_row = nc.dram_tensor("inverse_norms", [N], fp32, kind="Internal").ap()

    ctx = ExitStack()
    with ctx:
        def sb(name, shape, dt):
            return ctx.enter_context(nc.sbuf_tensor(name, shape, dt))

        def sem(name):
            return ctx.enter_context(nc.semaphore(name))

        adj_tb = sb("adj_t", [P, NS * T * ROWS], u8)
        x_sb = sb("x_sb", [P, T * D], fp32)
        table = sb("table", [P, T * TW], fp16)
        unit_t = sb("unit_t", [P, 2 * N], fp16)
        stage = sb("stage", [P, 2 * TPS * PW], fp32)
        adjm1b = sb("adjm1", [P, 2 * TPS * 2 * P], u8)
        e_hi = sb("e_hi", [P, 2 * 2 * ROWS], fp16)
        e_lo = sb("e_lo", [P, 2 * 2 * ROWS], fp16)
        inv_eps = sb("inv_eps", [P, T + 2], fp32)
        acc_sb = sb("acc_sb", [P, TPS * TW], fp32)
        small = sb("small", [P, 48], fp32)
        scales2 = sb("scales2", [P, 2 * T], fp32)
        mask_id = sb("mask_id", [P, P], bf16)
        mean_h = sb("mean_h", [P, D], fp32)
        ps = ctx.enter_context(nc.psum_tensor("ps", [P, 8, 512], fp32))

        adj_t = adj_tb[:, :].bitcast(fp8)
        adjm1 = adjm1b[:, :].bitcast(fp8)

        room = [0]

        def early(count, dt):
            size = count * (2 if dt == fp16 else 4)
            ap = adj_t[:, room[0]:room[0] + size].bitcast(dt)
            room[0] += size
            return ap

        u_f = early(T * D, fp32)
        h_f = early(T * D, fp32)
        stats = early(T * 6, fp32)
        mv = early(T * 2, fp32)
        ident = early(P, fp32)
        ones_w = early(P, fp16)
        var_e, rstd, scale_h, bias_h, norm2, norm2_g, rnorm = [early(T, fp32) for _ in range(7)]
        rnorm_s = early(T, fp32)
        neg_half = small[:, 32:40]
        c_scale = small[:, 40:44]
        c_minus = small[:, 44:48]

        h2_f = unit_t[:, :].bitcast(fp32)
        room2 = [0]

        def late(count, dt):
            size = count * (2 if dt == fp16 else 4) // 4
            ap = stage[:, room2[0]:room2[0] + size]
            room2[0] += size
            return ap if dt == fp32 else ap.bitcast(dt)

        w_in = late(2 * D, fp32)
        w_hi, w_lo = late(2 * D, fp16), late(2 * D, fp16)
        ident2 = late(P, fp16)
        neigh = late(ROWS, fp32)
        neigh_p = late(2 * ROWS, fp16)
        parts_t = late(4 * ROWS, fp16)
        max_inv = small[:, 9:10]
        max_inv_all = small[:, 10:11]
        small_norm = small[:, 11:12].bitcast(mybir.dt.int32)
        factor = e_lo[:, :].bitcast(fp32)
        beta = small[:, 0:1]
        beta_s = small[:, 1:2]
        exp_scale = small[:, 2:3]
        exp_bias = small[:, 3:4]
        b_sq = small[:, 4:5]
        b_zero = small[:, 5:6]
        b_inv = small[:, 6:7]
        b_keep = small[:, 7:8]
        b_pos = small[:, 8:9]
        no_edge = small[:, 12:16]
        den_s = small[:, 16:20]
        rden = small[:, 20:24]
        stats2 = small[:, 24:30]
        mv2 = small[:, 30:32]
        mean2 = scales2[:, 0:T]
        var2 = scales2[:, T:2 * T]

        def agg_bank(g):
            return 4 * ((g + 1) % 2)

        def post_bank(g):
            return agg_bank(g) if g < NS - 1 else agg_bank(g + 1)

        def out_bank(g, t):
            return post_bank(g) + (3 if g == NS - 1 and t == TPS - 1 else 2)

        def transpose_bank(g):
            return 4 + g if g < 4 else g - 4

        def tab(t, lo=0, hi=TW):
            return table[:, t * TW + lo:t * TW + hi]

        tab_v = table[:, :].rearrange("p (t w) -> p t w", w=TW)
        acc_v = acc_sb[:, :].rearrange("p (t w) -> p t w", w=TW)

        s_x = [sem(f"x_loaded{i}") for i in range(XP)]
        s_beta = sem("beta_loaded")
        s_w = sem("weights_loaded")
        s_stage = [sem(f"stage_loaded{i}") for i in range(2)]
        s_out = sem("out_stored")
        s_ident = sem("ident_ready")
        s_first = sem("constants_ready")
        s_maskid = sem("mask_identity_ready")
        s_step = sem("dve_step")
        s_var = sem("variance_ready")
        s_rstd = sem("rstd_ready")
        s_scales = sem("scales_ready")
        s_h = sem("h_ready")
        s_norm2 = sem("norm2_ready")
        s_rnorm = sem("rnorm_ready")
        s_rnorm_s = sem("rnorm_scaled")
        s_unit_p = sem("unit_by_gpsimd")
        s_unit_a = sem("unit_by_scalar")
        s_unit = sem("unit_by_vector")
        s_tp = sem("transposed")
        s_uhi = sem("unit_hi_ready")
        s_ulo = sem("unit_lo_ready")
        s_hh = sem("table_high_by_gpsimd")
        s_hh_act = sem("table_high_by_scalar")
        s_tab = sem("table_ready")
        s_adjm1 = sem("adjm1_ready")
        s_scores = sem("scores_ready")
        s_ehi = sem("exp_hi_ready")
        s_exp = sem("exp_ready")
        s_elo = sem("exp_lo_ready")
        s_adjt = sem("adj_t_ready")
        s_pvhi = sem("pv_high_done")
        s_pvlo = sem("pv_low_done")
        s_evac_v = sem("acc_evacuated_by_vector")
        s_evac_a = sem("acc_evacuated_by_scalar")
        s_rows = sem("rows_step")
        s_pool_waited = sem("pool_waited")
        s_dve_waited = sem("dve_waited")
        s_var2 = sem("variance2_ready")
        s_pool2 = sem("pool_step2")
        s_rs2 = sem("scales2_ready")
        s_h2 = sem("h2_ready")
        s_hh2 = sem("table2_high_ready")
        s_tab2 = sem("table2_low_by_vector")
        s_tab2_p = sem("table2_low_by_gpsimd")
        s_ident2 = sem("ident2_ready")
        s_max = sem("largest_inverse_norm_ready")
        s_flag = sem("small_norm_known")
        s_inv_stored = sem("inverse_norms_stored")
        s_inv = sem("inverse_norms_loaded")
        s_inv_eps = sem("scaled_inverse_norms_ready")
        s_factor = sem("factor_step")
        s_scaled = sem("scores_scaled")
        s_agg = sem("agg_ready")
        s_neigh = sem("neigh_ready")
        s_wsplit = sem("weights_split")
        s_post_t = sem("post_transposed")
        s_post_c = sem("post_copied")
        s_post_m = sem("post_multiplied")
        s_res = sem("result_ready")
        HIGH_BY_ACT = (2, 3)
        LOW_BY_POOL = (2, 3, 4)
        RS = 8
        CREDIT = 2
        ONE = 1

        block = ctx.enter_context(nc.Block())

        @block.sync
        def _(sp):
            sp.dma_start(beta, beta_in.partition_broadcast(P)).then_inc(s_beta, 16)
            for i in range(XP):
                sp.dma_start(x_sb[:, i * TX * D:(i + 1) * TX * D].rearrange("p (t d) -> p t d", d=D),
                             x_v[:, TX * i:TX * (i + 1), :]).then_inc(s_x[i], 16)
            with sp.Fori(0, NS) as s:
                with sp.Fori(0, PIECES // 2) as q:
                    for i in range(2):
                        sp.wait_ge(s_adjm1, s * PAIRS + q * 4 + (2 * i - 4 + 2 + CREDIT_ADJ))
                        sp.dma_start(stage[:, i * TPS * PW:(i + 1) * TPS * PW].rearrange("p (t c) -> p t c", c=PW),
                                     adj_v[:, bass.ds(s * TPS, TPS), bass.ds(q * 2 * PW + i * PW, PW)]
                                     ).then_inc(s_stage[i], 16)
            sp.wait_ge(s_adjm1, NS * PAIRS + CREDIT_ADJ)
            sp.dma_start(w_in[:, 0:D], w_neigh_in).then_inc(s_w, 16)
            sp.dma_start(w_in[:, D:2 * D], w_self_in).then_inc(s_w, 16)
            for g in range(NS - 1):
                sp.wait_ge(s_res, g + 1)
                sp.dma_start(out_v[:, g * TPS:(g + 1) * TPS, :],
                             x_sb[:, g * ROWS:(g + 1) * ROWS].rearrange("p (t d) -> p t d", d=D)).then_inc(s_out, 16)
            for a, b in ((T - TPS, T - 1), (T - 1, T)):
                sp.wait_ge(s_res, NS + 1 + b - (T - 1))
                sp.dma_start(out_v[:, a:b, :], x_sb[:, a * D:b * D].rearrange("p (t d) -> p t d", d=D)).then_inc(s_out, 16)
            sp.wait_ge(s_out, 16 * (NS + 1))

        @block.gpsimd
        def _(pool):
            pool.memset(c_scale, HS).then_inc(s_first, 1)
            pool.memset(c_minus, -1.0).then_inc(s_first, 1)
            pool.memset(neg_half, -0.5).then_inc(s_first, 1)
            pool.memset(ident, 0.0).then_inc(s_ident, 1)
            pool.memset(ones_w, 1.0).then_inc(s_first, 1)
            pool.memset(tab_v[:, :, 2 * D:TW], 1.0).then_inc(s_first, 1)
            pool.wait_ge(s_ident, 1)
            pool.affine_select(out=ident, in_=ident, compare_op=ALU.not_equal, fill=1.0, base=0,
                               pattern=[[-1, P]], channel_multiplier=1).then_inc(s_ident, 1)
            pool.wait_ge(s_first, 3)
            hv = h_f.rearrange("p (t d) -> p t d", d=D)

            def high_parts(g):
                pool.wait_ge(s_h, (g + 1) * TPS)
                pool.tensor_copy(tab_v[:, g * TPS:(g + 1) * TPS, D:2 * D], hv[:, g * TPS:(g + 1) * TPS, :]).then_inc(s_hh, 1)

            def low_parts(g):
                a, b = g * TPS, (g + 1) * TPS
                if g in HIGH_BY_ACT:
                    pool.wait_ge(s_hh_act, g - 1)
                else:
                    pool.wait_ge(s_hh, g + 1 if g < 2 else g - 1)
                pool.tensor_tensor(tab_v[:, a:b, 0:D], hv[:, a:b, :], tab_v[:, a:b, D:2 * D], ALU.subtract
                                   ).then_inc(s_tab, 1)

            def inverse_std(i):
                part = slice(i * TX, (i + 1) * TX)
                pool.wait_ge(s_var, i + 1)
                pool.tensor_tensor(rstd[:, part], var_e[:, part], neg_half, ALU.pow).then_inc(s_rstd, 1)

            def inverse_norm(i):
                part = slice(i * TX, (i + 1) * TX)
                pool.wait_ge(s_norm2, i + 1)
                pool.tensor_tensor(rnorm[:, part], norm2_g[:, part], neg_half, ALU.pow).then_inc(s_rnorm, 1)

            def scaled_inverse_norm(i):
                pool.wait_ge(s_rnorm, i + 1)
                pool.tensor_scalar(rnorm_s[:, i * TX:(i + 1) * TX], rnorm[:, i * TX:(i + 1) * TX], HS, None, ALU.mult
                                   ).then_inc(s_rnorm_s, 1)

            inverse_std(0)
            inverse_std(1)
            inverse_std(2)
            inverse_norm(0)
            scaled_inverse_norm(0)
            inverse_std(3)
            inverse_norm(1)
            pool.wait_ge(s_rnorm, 1)
            for t in range(TPS):
                pool.tensor_scalar(u_f[:, t * D:(t + 1) * D], h_f[:, t * D:(t + 1) * D], rnorm[:, t:t + 1], HS,
                                   ALU.mult, ALU.mult).then_inc(s_unit_p, 1)
            for i in range(2, XP):
                inverse_norm(i)
                if i == 2:
                    scaled_inverse_norm(2)

            def convert(u):
                slot, half = u // 2, u % 2
                src = stage[:, slot * TPS * PW:(slot + 1) * TPS * PW].rearrange("p (t c) -> p t c", c=PW)
                dst = adjm1b[:, half * TPS * 2 * P:(half + 1) * TPS * 2 * P].rearrange("p (t c) -> p t c", c=2 * P)
                pool.tensor_scalar(dst, src[:, :, half * 2 * P:(half + 1) * 2 * P], -FP8_MINUS_ONE, FP8_MINUS_ONE,
                                   ALU.mult, ALU.add).then_inc(s_adjm1, 1)

            h2_v = h2_f.rearrange("p (t d) -> p t d", d=D)

            def second_low(g):
                a, b = g * TPS, (g + 1) * TPS
                pool.wait_ge(s_hh2, g + 1)
                pool.tensor_tensor(tab_v[:, a:b, 0:D], h2_v[:, a:b, :], tab_v[:, a:b, D:2 * D], ALU.subtract
                                   ).then_inc(s_tab2_p, 1)

            def scales_of_x2(s):
                var, mean = var2[:, s * TPS:(s + 1) * TPS], mean2[:, s * TPS:(s + 1) * TPS]
                at = s * 3
                pool.wait_ge(s_var2, (s + 1) * TPS)
                pool.tensor_tensor(var, var, neg_half[:, 0:TPS], ALU.pow).then_inc(s_pool2, 1)
                pool.wait_ge(s_pool2, at + 1)
                pool.tensor_tensor(var, var, c_scale, ALU.mult).then_inc(s_pool2, 1)
                pool.wait_ge(s_pool2, at + 2)
                pool.tensor_tensor(mean, mean, var, ALU.mult).then_inc(s_pool2, 1)
                pool.wait_ge(s_pool2, at + 3)
                pool.tensor_tensor(mean, mean, c_minus, ALU.mult).then_inc(s_rs2, 1)

            for n in range(PAIRS):
                if n % 2 == 0:
                    pool.wait_ge(s_stage[n // 2 % 2], (n // UNROLL + 1) * 16)
                if n >= 2:
                    pool.wait_ge(s_scores, n - 1 + CREDIT)
                convert(n % UNROLL)
                if n == 1:
                    pool.wait_ge(s_max, 1)
                    pool.tensor_reduce(out=max_inv_all[0:1, :], in_=max_inv, axis=mybir.AxisListType.C, op=ALU.max
                                       ).then_inc(s_max, 1)
                    pool.wait_ge(s_max, 2)
                    pool.tensor_scalar(small_norm[0:1, :], max_inv_all[0:1, :], INV_PLAIN / HS, None, ALU.is_gt
                                       ).then_inc(s_flag, 1)
                if n in (1, 3) or (n >= 4 and n % 2 == 0):
                    g = n // 2
                    if g not in HIGH_BY_ACT:
                        high_parts(g)
                    low_parts(g)
            for s in range(1, NS):
                with pool.Fori(0, PAIRS // UNROLL) as k:
                    for u in range(UNROLL):
                        if u % 2 == 0:
                            pool.wait_ge(s_stage[u // 2], (k + (s * (PIECES // 2) + 1)) * 16)
                        pool.wait_ge(s_scores, k * UNROLL + (s * PAIRS + u - 1 + CREDIT))
                        pool.sem_inc(s_pool_waited, 1)
                        convert(u)
                if s >= 2:
                    scales_of_x2(s - 2)
            second_low(2)
            scales_of_x2(NS - 2)
            second_low(3)
            pool.wait_ge(s_adjm1, NS * PAIRS + CREDIT_ADJ)
            pool.memset(ident2, 0.0).then_inc(s_ident2, 1)
            pool.wait_ge(s_ident2, 1)
            pool.affine_select(out=ident2, in_=ident2, compare_op=ALU.not_equal, fill=1.0, base=0,
                               pattern=[[-1, P]], channel_multiplier=1).then_inc(s_ident2, 1)
            second_low(4)
            scales_of_x2(NS - 1)

        @block.scalar
        def _(act):
            act.preload_act_table(ACT.Exp)

            def unit_high(g):
                act.wait_ge(s_tp, g + 1)
                act.activation(unit_t[:, g * ROWS:(g + 1) * ROWS], ps[:, transpose_bank(g), :], ACT.Copy
                               ).then_inc(s_uhi, 1)

            for i in range(XP):
                act.wait_ge(s_scales, i + 1)
                for t in range(i * TX, (i + 1) * TX):
                    act.activation(h_f[:, t * D:(t + 1) * D], x_sb[:, t * D:(t + 1) * D], ACT.Relu,
                                   bias=bias_h[:, t:t + 1], scale=scale_h[:, t:t + 1]).then_inc(s_h, 1)
            act.wait_ge(s_h, T)
            for i, g in enumerate((1, 5)):
                act.wait_ge(s_rnorm_s, i + 1)
                for t in range(g * TPS, (g + 1) * TPS):
                    act.activation(u_f[:, t * D:(t + 1) * D], h_f[:, t * D:(t + 1) * D], ACT.Copy,
                                   scale=rnorm_s[:, t:t + 1]).then_inc(s_unit_a, 1)
            hv = h_f.rearrange("p (t d) -> p t d", d=D)

            def table_high(g):
                act.activation(tab_v[:, g * TPS:(g + 1) * TPS, D:2 * D], hv[:, g * TPS:(g + 1) * TPS, :], ACT.Copy
                               ).then_inc(s_hh_act, 1)

            for g in range(0, NS, 2):
                if g == 6:
                    act.wait_ge(s_flag, 1)
                    any_small = act.value_load(small_norm[0:1, :], min_val=0, max_val=1)
                unit_high(g)
                unit_high(g + 1)
                if g == 0:
                    for tg in HIGH_BY_ACT:
                        table_high(tg)

            def evacuate(s):
                act.wait_ge(s_pvlo, s * PAIRS + CREDIT)
                act.wait_ge(s_rows, s * (TPS * RS) + (ONE - 2))
                act.activation(acc_v[:, 2:TPS, :], ps[:, 2:TPS, 0:TW], ACT.Copy).then_inc(s_evac_a, 1)

            def load_inverse_norms(s, n, c, slot):
                if c == 0:
                    act.wait_ge(s_pvlo, n - 1 + CREDIT)
                else:
                    act.wait_ge(s_scaled, n * 2 + 1)
                act.dma_start(factor[:, slot * ROWS:(slot + 1) * ROWS],
                              inv_row[bass.ds(s * ROWS, ROWS)].partition_broadcast(P)).then_inc(s_inv, 16)

            def exps(s, k, evacuated, general, early_h2=None):
                for u in range(UNROLL):
                    n = s * PAIRS + k * UNROLL + u
                    bank = 4 + 2 * (u % 2)
                    hi = e_hi[:, (u % 2) * 2 * ROWS:(u % 2 + 1) * 2 * ROWS]
                    sc = ps[:, bank:bank + 2, :].rearrange("p a b -> p (a b)")
                    if u == 1 and evacuated:
                        evacuate(s)
                    if general:
                        for c in range(2):
                            load_inverse_norms(s, n, c, u % 2)
                        act.wait_ge(s_scaled, n * 2 + 2)
                    else:
                        act.wait_ge(s_scores, n + 1 + CREDIT)
                    act.wait_ge(s_pvhi, n - 1 + CREDIT)
                    act.wait_ge(s_adjt, n - 1 + CREDIT)
                    act.activation(hi, sc, ACT.Exp, bias=exp_bias, scale=exp_scale).then_inc(s_ehi, 1)
                    act.activation(sc, sc, ACT.Exp, bias=exp_bias, scale=exp_scale).then_inc(s_exp, 1)
                    if early_h2 is not None:
                        second_h(early_h2 * TPS + u)

            def second_h(t):
                if t % TPS == 0:
                    act.wait_ge(s_rs2, t // TPS + 1)
                act.activation(h2_f[:, t * D:(t + 1) * D], x_sb[:, t * D:(t + 1) * D], ACT.Relu,
                               bias=mean2[:, t:t + 1], scale=var2[:, t:t + 1]).then_inc(s_h2, 1)

            def all_exps(general):
                with act.Fori(0, PAIRS // UNROLL) as k:
                    exps(0, k, False, general)
                with act.Fori(1, NS - 1) as s:
                    exps(s, 0, True, general)
                    with act.Fori(1, PAIRS // UNROLL) as k:
                        exps(s, k, False, general)
                for k in range(PAIRS // UNROLL):
                    exps(NS - 1, k, k == 0, general, early_h2=k - 2 if k >= 2 else None)

            with act.If(any_small < 1):
                all_exps(False)
            with act.If(any_small > 0):
                act.wait_ge(s_rnorm, XP)
                act.dma_start(inv_row.rearrange("(t p) -> p t", p=P), rnorm, allow_slow_non_contiguous=True
                              ).then_inc(s_inv_stored, 16)
                act.wait_ge(s_inv_stored, 16)
                all_exps(True)

            for t in range(2 * TPS, T):
                if t == 3 * TPS:
                    evacuate(NS)
                second_h(t)
            for g in range(NS):
                b0 = post_bank(g)
                if g >= 1:
                    act.wait_ge(s_post_m, g)
                for i in range(2 if g < NS - 1 else 1):
                    act.wait_ge(s_post_t, 2 * g + i + 1)
                    act.activation(parts_t[:, i * 2 * ROWS:(i + 1) * 2 * ROWS], ps[:, b0 + i, :].bitcast(fp16), ACT.Copy
                                   ).then_inc(s_post_c, 1)

            for i, own in enumerate((slice(0, 2 * P), slice(2 * P, 3 * P), slice(3 * P, 4 * P))):
                act.wait_ge(s_post_t, 2 * NS + i)
                act.activation(parts_t[:, 2 * ROWS:4 * ROWS].rearrange("p (a c) -> p a c", a=2)[:, :, own],
                               ps[:, post_bank(NS - 1) + 1, :].bitcast(fp16).rearrange("p (a c) -> p a c", a=2)[:, :, own],
                               ACT.Copy).then_inc(s_post_c, 1)

        @block.vector
        def _(dve):
            steps = [0]

            def then(ins):
                steps[0] += 1
                ins.then_inc(s_step, 1)
                dve.wait_ge(s_step, steps[0])

            mv_v = mv.rearrange("p (t c) -> p t c", c=2)

            def variances(i):
                dve.wait_ge(s_x[i], 16)
                for t in range(i * TX, (i + 1) * TX):
                    last = dve.bn_stats(stats[:, t * 6:(t + 1) * 6], x_sb[:, t * D:(t + 1) * D])
                then(last)
                for t in range(i * TX, (i + 1) * TX):
                    last = dve.bn_aggr(mv[:, t * 2:(t + 1) * 2], stats[:, t * 6:(t + 1) * 6])
                then(last)
                dve.tensor_scalar(var_e[:, i * TX:(i + 1) * TX], mv_v[:, i * TX:(i + 1) * TX, 1], EPS, None,
                                  ALU.add).then_inc(s_var, 1)

            def scales(i):
                part = slice(i * TX, (i + 1) * TX)
                dve.wait_ge(s_rstd, i + 1)
                then(dve.tensor_scalar(scale_h[:, part], rstd[:, part], HS, None, ALU.mult))
                dve.scalar_tensor_tensor(bias_h[:, part], mv_v[:, part, 0], -1.0, scale_h[:, part],
                                         ALU.mult, ALU.mult).then_inc(s_scales, 1)

            def norms(i):
                part = slice(i * TX, (i + 1) * TX)
                for t in range(i * TX, (i + 1) * TX):
                    dve.wait_ge(s_h, t + 1)
                    last = dve.tensor_tensor_reduce(
                        out=u_f[:, t * D:(t + 1) * D], in0=h_f[:, t * D:(t + 1) * D], in1=h_f[:, t * D:(t + 1) * D],
                        scale=1.0, scalar=0.0, op0=ALU.mult, op1=ALU.add, accum_out=norm2[:, t:t + 1])
                then(last)
                dve.tensor_scalar(norm2_g[:, part], norm2[:, part], 1e-20, None, ALU.max).then_inc(s_norm2, 1)

            def units(i, tiles=TX):
                dve.wait_ge(s_rnorm, i + 1)
                for t in range(i * TX, i * TX + tiles):
                    dve.tensor_scalar(u_f[:, t * D:(t + 1) * D], h_f[:, t * D:(t + 1) * D], rnorm[:, t:t + 1], HS,
                                      ALU.mult, ALU.mult).then_inc(s_unit, 1)

            def unit_low(g):
                dve.wait_ge(s_uhi, g + 1)
                dve.tensor_tensor(unit_t[:, N + g * ROWS:N + (g + 1) * ROWS], ps[:, transpose_bank(g), :],
                                  unit_t[:, g * ROWS:(g + 1) * ROWS], ALU.subtract).then_inc(s_ulo, 1)

            dve.sem_inc(s_adjm1, CREDIT_ADJ)
            dve.sem_inc(s_pvhi, CREDIT)
            dve.sem_inc(s_pvlo, CREDIT)
            dve.sem_inc(s_adjt, CREDIT)
            dve.sem_inc(s_elo, CREDIT)
            dve.sem_inc(s_scores, CREDIT)
            dve.sem_inc(s_rows, TPS * RS + ONE)
            dve.wait_ge(s_beta, 16)
            then(dve.tensor_tensor(b_sq, beta, beta, ALU.mult))
            then(dve.tensor_scalar(b_zero, b_sq, 1e-36, 1e-18, ALU.is_le, ALU.mult))
            then(dve.tensor_scalar(b_keep, b_sq, 1e-36, None, ALU.is_gt))
            then(dve.scalar_tensor_tensor(beta_s, beta, b_keep, b_zero, ALU.mult, ALU.add))
            then(dve.reciprocal(b_inv, beta_s))
            then(dve.tensor_scalar(exp_scale, beta_s, 1.0 / (HS * HS), None, ALU.mult))
            then(dve.tensor_scalar(b_pos, beta, 0.0, None, ALU.max))
            then(dve.tensor_scalar(exp_bias, b_pos, -1.0, E_BITS * LN2, ALU.mult, ALU.add))
            dve.wait_ge(s_ident, 2)
            dve.tensor_scalar(mask_id[:, :], ident, b_inv, MASK * HS * HS, ALU.mult, ALU.mult).then_inc(s_maskid, 1)
            variances(0)
            variances(1)
            scales(0)
            variances(2)
            scales(1)
            norms(0)
            scales(2)
            variances(3)
            norms(1)
            scales(3)
            norms(2)
            units(1)
            norms(3)
            units(2, TPS)
            unit_low(0)
            units(3)
            dve.tensor_reduce(out=max_inv, in_=rnorm, axis=mybir.AxisListType.X, op=ALU.max).then_inc(s_max, 1)
            unit_low(1)
            unit_low(2)
            unit_low(3)
            dve.wait_ge(s_flag, 1)
            any_small = dve.value_load(small_norm[0:1, :], min_val=0, max_val=1)
            for g in range(4, NS):
                unit_low(g)
            dve.sem_inc(s_evac_v, ONE)
            dve.sem_inc(s_evac_a, ONE)

            def finish_rows(step, done, x_row, acc, at, mean_dst, var_dst):
                def after(i):
                    dve.wait_ge(s_rows, at + i + ONE)

                ne, den, r = no_edge[:, 0:1], den_s[:, 0:1], rden[:, 0:1]
                if step == 0:
                    dve.wait_ge(s_evac_v, done + ONE)
                    dve.wait_ge(s_evac_a, done + ONE)
                    dve.tensor_scalar(ne, acc(2 * D, 1), 0.0, None, ALU.is_equal).then_inc(s_rows, 1)
                    after(1)
                    dve.scalar_tensor_tensor(den, acc(2 * D, 1), HS, ne, ALU.mult, ALU.add).then_inc(s_rows, 1)
                    after(2)
                    dve.reciprocal(r, den).then_inc(s_rows, 1)
                if step == 1:
                    after(3)
                    dve.scalar_tensor_tensor(x_row, acc(0, D), r, x_row, ALU.mult, ALU.add).then_inc(s_rows, 1)
                if step == 2:
                    after(4)
                    dve.scalar_tensor_tensor(x_row, acc(D, D), r, x_row, ALU.mult, ALU.add).then_inc(s_rows, 1)
                    after(5)
                    dve.scalar_tensor_tensor(x_row, mean_h[:, :], ne, x_row, ALU.mult, ALU.add).then_inc(s_rows, 1)
                if step == 3:
                    after(6)
                    dve.sem_inc(s_dve_waited, 1)
                    dve.bn_stats(stats2, x_row).then_inc(s_rows, 1)
                    after(7)
                    dve.sem_inc(s_dve_waited, 1)
                    dve.bn_aggr(mv2, stats2).then_inc(s_rows, 1)
                    after(8)
                    dve.tensor_copy(mean_dst, mv2[:, 0:1])
                    dve.tensor_scalar(var_dst, mv2[:, 1:2], EPS, None, ALU.add).then_inc(s_var2, 1)

            def transposed_edges(at, slot, pairs_before):
                dve.wait_ge(s_ehi, pairs_before + 1)
                dve.tensor_scalar(adj_tb[:, at], e_hi[:, slot * 2 * ROWS:(slot + 1) * 2 * ROWS], 0.0, FP8_ONE,
                                  ALU.is_gt, ALU.mult).then_inc(s_adjt, 1)

            h2_v = h2_f.rearrange("p (t d) -> p t d", d=D)

            def second_table(g):
                a, b = g * TPS, (g + 1) * TPS
                dve.wait_ge(s_h2, (g + 1) * TPS)
                dve.tensor_copy(tab_v[:, a:b, D:2 * D], h2_v[:, a:b, :]).then_inc(s_hh2, 1)
                if g in LOW_BY_POOL:
                    return
                dve.wait_ge(s_hh2, g + 1)
                dve.tensor_tensor(tab_v[:, a:b, 0:D], h2_v[:, a:b, :], tab_v[:, a:b, D:2 * D], ALU.subtract
                                  ).then_inc(s_tab2, 1)

            def scale_scores(s, pair, slot):
                n = s * PAIRS + pair
                f = factor[:, slot * ROWS:(slot + 1) * ROWS]
                for c in range(2):
                    dve.wait_ge(s_inv, (n * 2 + (c + 1)) * 16)
                    if c == 0:
                        dve.wait_ge(s_scores, n + 1 + CREDIT)
                    dve.tensor_scalar(f, f, inv_eps[:, bass.ds(pair * 2 + c, 1)], 1.0, ALU.mult, ALU.add
                                      ).then_inc(s_factor, 1)
                    dve.wait_ge(s_factor, n * 6 + (3 * c + 1))
                    dve.tensor_scalar(f, f, FACTOR_MAX, None, ALU.min).then_inc(s_factor, 1)
                    dve.wait_ge(s_factor, n * 6 + (3 * c + 2))
                    dve.reciprocal(f, f).then_inc(s_factor, 1)
                    dve.wait_ge(s_factor, n * 6 + (3 * c + 3))
                    bank = 4 + 2 * slot + c
                    dve.tensor_tensor(ps[:, bank, :], ps[:, bank, :], f, ALU.mult).then_inc(s_scaled, 1)

            def four_pairs(s, k, general, first=False, last=False):
                for u in range(UNROLL):
                    n = s * PAIRS + k * UNROLL + u
                    bank = 4 + 2 * (u % 2)
                    sl = slice((u % 2) * 2 * ROWS, (u % 2 + 1) * 2 * ROWS)
                    dve.wait_ge(s_exp, n + 1)
                    dve.wait_ge(s_pvlo, n - 1 + CREDIT)
                    dve.tensor_tensor(e_lo[:, sl], ps[:, bank:bank + 2, :].rearrange("p a b -> p (a b)"),
                                      e_hi[:, sl], ALU.subtract).then_inc(s_elo, 1)
                    if last and u == 1:
                        second_table(0)
                    if last and u == UNROLL - 1:
                        second_table(1)
                        evacuate(s)
                        second_table(2)
                    if not first:
                        finish_rows(u, s, x_sb[:, bass.ds((s - 1) * ROWS + k * D, D)],
                                    lambda at, size: acc_sb[:, bass.ds(k * TW + at, size)],
                                    (s * TPS + k) * RS, mean2[:, bass.ds((s - 1) * TPS + k, 1)],
                                    var2[:, bass.ds((s - 1) * TPS + k, 1)])
                    if not (last and u == UNROLL - 1):
                        if general and u < UNROLL - 1:
                            scale_scores(s, k * UNROLL + (u + 1), (u + 1) % 2)
                        elif general:
                            scale_scores(s, k * UNROLL + UNROLL, 0)
                        transposed_edges(bass.ds(s * T * ROWS + k * UNROLL * 2 * ROWS + (u + 1) * 2 * ROWS, 2 * ROWS),
                                         (u + 1) % 2, n + 1)

            def evacuate(s):
                dve.wait_ge(s_pvlo, s * PAIRS + (PAIRS + CREDIT))
                dve.tensor_copy(acc_v[:, 0:2, :], ps[:, 0:2, 0:TW]).then_inc(s_evac_v, 1)

            def attention(general):
                if general:
                    scale_scores(0, 0, 0)
                transposed_edges(slice(0, 2 * ROWS), 0, 0)
                with dve.Fori(0, PAIRS // UNROLL) as k:
                    four_pairs(0, k, general, first=True)
                dve.wait_ge(s_pvlo, PAIRS + CREDIT)
                dve.tensor_scalar(mean_h[:, :], ps[:, 0, 3 * D:4 * D], 1.0 / (HS * N), None, ALU.mult)
                evacuate(0)
                with dve.Fori(1, NS - 1) as s:
                    with dve.Fori(0, PAIRS // UNROLL) as k:
                        four_pairs(s, k, general)
                    evacuate(s)
                with dve.Fori(0, PAIRS // UNROLL - 1) as k:
                    four_pairs(NS - 1, k, general)
                four_pairs(NS - 1, PAIRS // UNROLL - 1, general, last=True)

            with dve.If(any_small < 1):
                attention(False)
            with dve.If(any_small > 0):
                dve.wait_ge(s_rnorm, XP)
                dve.tensor_scalar(inv_eps[:, 0:T], rnorm, EPS_COS * HS * HS, None, ALU.mult).then_inc(s_inv_eps, 1)
                dve.tensor_scalar(inv_eps[:, T:T + 2], rnorm[:, 0:2], EPS_COS * HS * HS, None, ALU.mult
                                  ).then_inc(s_inv_eps, 1)
                dve.wait_ge(s_inv_eps, 2)
                attention(True)
            last_rows = [x_sb[:, (T - TPS + t) * D:(T - TPS + t + 1) * D] for t in range(TPS)]
            dve.wait_ge(s_evac_v, NS + ONE)
            dve.wait_ge(s_evac_a, NS + ONE)
            then(dve.tensor_scalar(no_edge, acc_v[:, :, 2 * D], 0.0, None, ALU.is_equal))
            then(dve.scalar_tensor_tensor(den_s, acc_v[:, :, 2 * D], HS, no_edge, ALU.mult, ALU.add))
            then(dve.reciprocal(rden, den_s))
            second_table(3)
            for t in range(TPS):
                last = dve.scalar_tensor_tensor(last_rows[t], acc_v[:, t, 0:D], rden[:, t:t + 1], last_rows[t],
                                                ALU.mult, ALU.add)
            then(last)
            second_table(4)
            for t in range(TPS):
                last = dve.scalar_tensor_tensor(last_rows[t], acc_v[:, t, D:2 * D], rden[:, t:t + 1], last_rows[t],
                                                ALU.mult, ALU.add)
            then(last)
            for t in range(TPS):
                last = dve.scalar_tensor_tensor(last_rows[t], mean_h[:, :], no_edge[:, t:t + 1], last_rows[t],
                                                ALU.mult, ALU.add)
            then(last)
            last_st = acc_sb[:, 0:TPS * 6]
            last_mv = acc_sb[:, TPS * 6:TPS * 8].rearrange("p (t c) -> p t c", c=2)
            for t in range(TPS):
                last = dve.bn_stats(last_st[:, t * 6:(t + 1) * 6], last_rows[t])
            then(last)
            for t in range(TPS):
                last = dve.bn_aggr(last_mv[:, t, :], last_st[:, t * 6:(t + 1) * 6])
            then(last)
            then(dve.tensor_copy(mean2[:, T - TPS:T], last_mv[:, :, 0]))
            dve.tensor_scalar(var2[:, T - TPS:T], last_mv[:, :, 1], EPS, None, ALU.add).then_inc(s_var2, TPS)
            for g in range(5, NS):
                second_table(g)
            dve.wait_ge(s_w, 32)
            then(dve.tensor_scalar(w_hi, w_in, WS, None, ALU.mult))
            dve.scalar_tensor_tensor(w_lo, w_in, WS, w_hi, ALU.mult, ALU.subtract).then_inc(s_wsplit, 1)
            xg = x_sb[:, :].rearrange("p (g r) -> p g r", r=ROWS)

            def result(g, cols, products):
                dve.wait_ge(s_post_m, products)
                bank = out_bank(g, cols.start // D)
                dve.scalar_tensor_tensor(xg[:, g, cols], ps[:, bank, cols], 1.0 / (HS * WS), xg[:, g, cols],
                                         ALU.mult, ALU.add).then_inc(s_res, 1)

            for g in range(NS - 1):
                b0 = agg_bank(g)
                dve.wait_ge(s_agg, g + 1)
                then(dve.tensor_scalar(den_s, ps[:, b0:b0 + 4, 2 * D], 1.0, None, ALU.max))
                then(dve.reciprocal(rden, den_s))
                for t in range(TPS):
                    last = dve.tensor_scalar(neigh[:, t * D:(t + 1) * D], ps[:, b0 + t, 0:D], rden[:, t:t + 1], None,
                                             ALU.mult)
                then(last)
                for t in range(TPS):
                    last = dve.scalar_tensor_tensor(neigh[:, t * D:(t + 1) * D], ps[:, b0 + t, D:2 * D],
                                                    rden[:, t:t + 1], neigh[:, t * D:(t + 1) * D], ALU.mult, ALU.add)
                then(last)
                then(dve.tensor_copy(neigh_p[:, 0:ROWS], neigh))
                dve.tensor_tensor(neigh_p[:, ROWS:2 * ROWS], neigh, neigh_p[:, 0:ROWS], ALU.subtract
                                  ).then_inc(s_neigh, 1)
                if g < NS - 2:
                    result(g, slice(0, ROWS), g + 1)
            g = NS - 1
            for t in range(TPS):
                own, low = slice(t * D, (t + 1) * D), slice(ROWS + t * D, ROWS + (t + 1) * D)
                bank = agg_bank(g) + t
                dve.wait_ge(s_agg, g + t + 1)
                then(dve.tensor_scalar(den_s[:, t:t + 1], ps[:, bank, 2 * D:TW], 1.0, None, ALU.max))
                then(dve.reciprocal(rden[:, t:t + 1], den_s[:, t:t + 1]))
                then(dve.tensor_scalar(neigh[:, own], ps[:, bank, 0:D], rden[:, t:t + 1], None, ALU.mult))
                then(dve.scalar_tensor_tensor(neigh[:, own], ps[:, bank, D:2 * D], rden[:, t:t + 1], neigh[:, own],
                                              ALU.mult, ALU.add))
                if t == 0:
                    dve.wait_ge(s_post_t, 2 * g)
                then(dve.tensor_copy(neigh_p[:, own], neigh[:, own]))
                dve.tensor_tensor(neigh_p[:, low], neigh[:, own], neigh_p[:, own], ALU.subtract).then_inc(s_neigh, 1)
                if t == 1:
                    result(g - 1, slice(0, ROWS), g)
                if t == 2:
                    result(g, slice(0, 2 * D), g + 1)
            result(g, slice(2 * D, 3 * D), g + 2)
            result(g, slice(3 * D, 4 * D), g + 3)

        @block.tensor
        def _(pe):
            pe.wait_ge(s_ident, 2)

            def unit_transpose(g):
                if g == 0:
                    pe.wait_ge(s_unit_p, TPS)
                elif g in (1, 5):
                    pe.wait_ge(s_unit_a, TPS if g == 1 else 2 * TPS)
                else:
                    pe.wait_ge(s_unit, (g - 1 if g < 5 else g - 2) * TPS)
                for t in range(TPS):
                    at = (g * TPS + t) * D
                    last = pe.transpose(ps[:, transpose_bank(g), t * P:(t + 1) * P], u_f[:, at:at + D], ident)
                last.then_inc(s_tp, 1)

            def scores(s, pair, par, n):
                pe.wait_ge(s_elo, n - 1 + CREDIT)
                pe.wait_ge(s_adjm1, n + 1 + CREDIT_ADJ)
                for c in range(2):
                    dst = ps[:, 4 + 2 * par + c, :]
                    ch = pair * (2 * P) + c * P
                    hi_j, lo_j = unit_t[:, bass.ds(ch, P)], unit_t[:, bass.ds(N + ch, P)]
                    hi_i, lo_i = unit_t[:, bass.ds(s * ROWS, ROWS)], unit_t[:, bass.ds(N + s * ROWS, ROWS)]
                    pe.matmul(dst, lo_j, hi_i, start=True, stop=False)
                    pe.matmul(dst, hi_j, lo_i, start=False, stop=False)
                    pe.matmul(dst, hi_j, hi_i, start=False, stop=False)
                    for t in range(TPS):
                        at = (par * TPS + t) * 2 * P + c * P
                        last = pe.matmul(dst[:, t * P:(t + 1) * P], adjm1[:, at:at + P], mask_id[:, :],
                                         start=False, stop=(t == TPS - 1))
                last.then_inc(s_scores, 1)

            def attend(part, pair, par, n, start=False, end=False):
                high = part is e_hi
                lo = 0 if high else D
                if high:
                    pe.wait_ge(s_ehi, n + 1)
                else:
                    pe.wait_ge(s_elo, n + 1 + CREDIT)
                for c in range(2):
                    mov = table[:, bass.ds((pair * 2 + c) * TW + lo, TW - lo)]
                    for t in range(TPS):
                        at = par * 2 * ROWS + c * ROWS + t * P
                        last = pe.matmul(ps[:, t, lo:TW], part[:, at:at + P], mov,
                                         start=start and c == 0, stop=end and c == 1)
                last.then_inc(s_pvhi if high else s_pvlo, 1)

            for g in range(NS):
                unit_transpose(g)
            pe.wait_ge(s_ulo, 2)
            pe.wait_ge(s_maskid, 1)
            scores(0, 0, 0, 0)
            pe.wait_ge(s_ulo, 4)
            pe.wait_ge(s_first, 5)

            with pe.Fori(0, NS) as s:
                def body(k, first, end):
                    for u in range(UNROLL):
                        n = s * PAIRS + k * UNROLL + u
                        if not (end and u == UNROLL - 1):
                            if u % 2 == 1:
                                pe.wait_ge(s_ulo, k * 2 + ((u + 1) // 2 + 1))
                            scores(s, k * UNROLL + (u + 1), (u + 1) % 2, n + 1)
                        else:
                            with pe.If(s < NS - 1):
                                scores(nc.s_assert_within(s + 1, 1, NS - 1, skip_runtime_bounds_check_because=
                                    "the branch is not taken in the last supertile"), 0, 0, n + 1)
                        if first and u == 0:
                            pe.wait_ge(s_ulo, NS)
                            pe.wait_ge(s_evac_v, s + ONE)
                            pe.wait_ge(s_evac_a, s + ONE)
                        if u % 2 == 0:
                            pe.wait_ge(s_tab, k * 2 + (u // 2 + 1))
                        attend(e_hi, k * UNROLL + u, u % 2, n, start=first and u == 0)
                        if not (first and u == 0):
                            attend(e_lo, k * UNROLL + (u - 1), (u - 1) % 2, n - 1)
                    if end:
                        with pe.If(s < 1):
                            for t in range(T):
                                for lo in (0, D):
                                    pe.matmul(ps[:, 0, 3 * D:4 * D], ones_w[:, :], tab(t, lo, lo + D),
                                              start=False, stop=False, skip_group_check=True)
                        attend(e_lo, PAIRS - 1, (PAIRS - 1) % 2, n, end=True)

                body(0, True, False)
                with pe.Fori(1, PAIRS // UNROLL - 1) as k:
                    body(k, False, False)
                body(PAIRS // UNROLL - 1, False, True)

            def transpose_parts(g, which, tiles):
                dst = ps[:, post_bank(g) + which, :].bitcast(fp16)
                for part in range(2):
                    for t in tiles:
                        if which == 1:
                            src = neigh_p[:, part * ROWS + t * D:part * ROWS + (t + 1) * D]
                        else:
                            src = tab(g * TPS + t, D - part * D, 2 * D - part * D)
                        at = part * ROWS + t * P
                        last = pe.transpose(dst[:, at:at + P], src, ident2)
                last.then_inc(s_post_t, 1)

            def multiply_parts(g, which, tiles):
                w = slice(D - which * D, 2 * D - which * D)
                for t in tiles:
                    at = which * 2 * ROWS + t * P
                    high, low = parts_t[:, at:at + P], parts_t[:, at + ROWS:at + ROWS + P]
                    for i, (a, b) in enumerate(((low, w_hi), (high, w_lo), (high, w_hi))):
                        new_bank = t == 0 or out_bank(g, t) != out_bank(g, t - 1)
                        last = pe.matmul(ps[:, out_bank(g, t), t * P:(t + 1) * P], a, b[:, w],
                                         start=(which == 0 and new_bank and i == 0), stop=(which == 1 and i == 2),
                                         skip_group_check=True)
                if which == 1:
                    last.then_inc(s_post_m, 1)

            ALL = range(TPS)
            pe.wait_ge(s_adjt, NS * PAIRS + CREDIT)

            def aggregate(g, t, b):
                at = (g * T + b) * ROWS + t * P
                return pe.matmul(ps[:, agg_bank(g) + t, 0:TW], adj_t[:, at:at + P], tab(b), start=(b == 0),
                                 stop=(b == T - 1))

            for g in range(NS - 1):
                if g == 1:
                    pe.wait_ge(s_evac_v, NS + ONE)
                    pe.wait_ge(s_evac_a, NS + ONE)
                if g >= 2:
                    pe.wait_ge(s_res, g - 1)
                for b in range(T):
                    if g == 0 and b % TPS == 0:
                        by_pool = sum(i in LOW_BY_POOL for i in range(b // TPS + 1))
                        if b // TPS in LOW_BY_POOL:
                            pe.wait_ge(s_tab2_p, by_pool)
                        else:
                            pe.wait_ge(s_tab2, b // TPS + 1 - by_pool)
                    for t in ALL:
                        last = aggregate(g, t, b)
                    if g >= 1 and b == T // 4:
                        if g == 1:
                            pe.wait_ge(s_ident2, 2)
                            pe.wait_ge(s_wsplit, 1)
                        pe.wait_ge(s_neigh, g)
                        transpose_parts(g - 1, 0, ALL)
                        transpose_parts(g - 1, 1, ALL)
                    if g >= 1 and b == T // 2:
                        pe.wait_ge(s_post_c, 2 * g)
                        multiply_parts(g - 1, 0, ALL)
                        multiply_parts(g - 1, 1, ALL)
                last.then_inc(s_agg, 1)
            g = NS - 1
            pe.wait_ge(s_res, g - 1)
            for t in ALL:
                for b in range(T):
                    last = aggregate(g, t, b)
                    if t == 1 and b == T // 4:
                        pe.wait_ge(s_neigh, g)
                        transpose_parts(g - 1, 0, ALL)
                        transpose_parts(g - 1, 1, ALL)
                    if t == 2 and b == T // 8:
                        pe.wait_ge(s_post_c, 2 * g)
                        multiply_parts(g - 1, 0, ALL)
                        multiply_parts(g - 1, 1, ALL)
                        transpose_parts(g, 0, ALL)
                    if t == 2 and b == T * 3 // 4:
                        pe.wait_ge(s_neigh, g + 2)
                        transpose_parts(g, 1, [0, 1])
                    if t == 2 and b == T - 1:
                        pe.wait_ge(s_res, g)
                        pe.wait_ge(s_post_c, 2 * g + 1)
                        multiply_parts(g, 0, ALL)
                    if t == 3 and b == T // 4:
                        pe.wait_ge(s_post_c, 2 * g + 2)
                        multiply_parts(g, 1, [0, 1])
                    if t == 3 and b == T * 5 // 8:
                        pe.wait_ge(s_neigh, g + 3)
                        transpose_parts(g, 1, [2])
                    if t == 3 and b == T - 2:
                        pe.wait_ge(s_post_c, 2 * g + 3)
                        pe.wait_ge(s_res, g + 1)
                        multiply_parts(g, 1, [2])
                last.then_inc(s_agg, 1)
            pe.wait_ge(s_neigh, g + 4)
            transpose_parts(g, 1, [3])
            pe.wait_ge(s_post_c, 2 * g + 4)
            multiply_parts(g, 1, [3])


_INS = ["x", "adj", "L0_gnn_beta", "L1_gnn_W_self", "L1_gnn_W_neigh"]


def kernel(**inputs):
    import numpy as _np
    import concourse.bacc as _bacc
    from concourse import mybir as _mybir
    from concourse.bass_utils import run_bass_kernel_spmd as _run

    nc = _bacc.Bacc("TRN2", target_bir_lowering=False, num_devices=1)
    arrays, args = {}, []
    for name in _INS:
        a = _np.ascontiguousarray(inputs[name])
        arrays[f"in_{name}_dram"] = a
        args.append(nc.dram_tensor(f"in_{name}_dram", a.shape, _mybir.dt.from_np(a.dtype), kind="ExternalInput").ap())
    shape = inputs["x"].shape
    args.append(nc.dram_tensor("out_0_dram", shape, _mybir.dt.float32, kind="ExternalOutput").ap())
    gnn_program(nc, *args)
    r = _run(nc, [arrays], core_ids=[0])
    return r.results[0]["out_0_dram"]
```
